# Optimizing a Trainium2 kernel written in Bass

```python
import numpy as np
import jax
import jax.numpy as jnp

def _softmax(x, axis=-1):
    return jax.nn.softmax(x, axis=axis)
def _gelu(x):
    return jax.nn.gelu(x, approximate=True)
def _silu(x):
    return jax.nn.silu(x)
def _sigmoid(x):
    return jax.nn.sigmoid(x)
def _layernorm(x, axis=-1, eps=1e-5):
    m = jnp.mean(x, axis=axis, keepdims=True)
    v = jnp.var(x, axis=axis, keepdims=True)
    return (x - m) / jnp.sqrt(v + eps)
def _scatter_add(tgt, idx, src, axis=0):
    return tgt.at[idx].add(src)
def _segment_sum(src, seg, n):
    return jax.ops.segment_sum(src, seg, n)

kernel_name = 'mk_conv_attn_hybrid_d4_conv_nchw128_0f295e'

def setup_inputs(seed: int = 0):
    np.random.seed(seed)
    _w = jnp.asarray
    def _rec_inputs():
        import jax
        import jax.numpy as jnp
        _gk = jax.random.key(seed)
        x = -0.0009896 + 1 * jax.random.normal(jax.random.fold_in(_gk, 1), (16, 128, 28, 28), jnp.float32)
        return x
    x = _rec_inputs()
    def _L0_conv_setup():
        import jax, jax.numpy as jnp
        import numpy as np
        B, C, H, W_SP = (16, 128, 28, 28)
        F, KS, STRIDE, PAD = (128, 3, 1, 1)
        CHUNK = 4
        EPS = 1e-12

        def _patches(x):
            p = jax.lax.conv_general_dilated_patches(x, (KS, KS), (STRIDE, STRIDE), [(PAD, PAD), (PAD, PAD)], dimension_numbers=('NCHW', 'OIHW', 'NCHW'))
            b, k, ho, wo = p.shape
            return (p.reshape(b, k, ho * wo), ho, wo)
        key = jax.random.key(seed)
        kx, kw = jax.random.split(key)
        x = jax.random.normal(kx, (B, C, H, W_SP), dtype=jnp.float32)
        std = float(np.sqrt(2.0 / (C * KS * KS)))
        W = jax.random.normal(kw, (F, C, KS, KS), dtype=jnp.float32) * std
        return {'x': x, 'W': W}
    _L0_conv_all = _L0_conv_setup()
    _L0_conv_in = {k: v for k, v in _L0_conv_all.items() if k in ('W', )}
    del _L0_conv_all

    def _L1_conv_setup():
        import jax, jax.numpy as jnp
        import numpy as np
        A_BIT = 4
        W_BIT = 4
        EPS = 1e-05
        L_TH = 2

        def _pattern_mask():
            m = np.ones((3, 3), np.float32)
            m[0, 0] = 0.0
            m[2, 2] = 0.0
            return jnp.asarray(m)

        def ste_round(x):
            return x + jax.lax.stop_gradient(jnp.round(x) - x)

        def qfn(x, k):
            n = float(2 ** k - 1)
            return ste_round(x * n) / n

        def act_quant(x, k):
            return qfn(jnp.clip(x, 0.0, 1.0), k)

        def weight_quant(w, k):
            t = jnp.tanh(w)
            t = t / (2.0 * jnp.max(jnp.abs(t))) + 0.5
            return 2.0 * qfn(t, k) - 1.0

        def bn_eval(x, gamma, beta, mean, var):
            inv = gamma / jnp.sqrt(var + EPS)
            return x * inv[None, :, None, None] + (beta - mean * inv)[None, :, None, None]

        def conv3x3(x, w):
            return jax.lax.conv_general_dilated(x, w, window_strides=(1, 1), padding=[(1, 1), (1, 1)], dimension_numbers=('NCHW', 'OIHW', 'NCHW'))
        key = jax.random.key(seed)
        ks = jax.random.split(key, 8)
        B, C, H, W = (128, 128, 32, 32)
        x = jax.random.normal(ks[0], (B, C, H, W), jnp.float32)
        w1 = jax.random.normal(ks[1], (C, C, 3, 3), jnp.float32) * 0.05
        w2 = jax.random.normal(ks[2], (C, C, 3, 3), jnp.float32) * 0.05
        gamma1 = jnp.ones((C,), jnp.float32)
        beta1 = jnp.zeros((C,), jnp.float32)
        mean1 = jax.random.normal(ks[3], (C,), jnp.float32) * 0.1
        var1 = jax.random.uniform(ks[4], (C,), jnp.float32, 0.5, 1.5)
        gamma2 = jnp.ones((C,), jnp.float32)
        beta2 = jnp.zeros((C,), jnp.float32)
        mean2 = jax.random.normal(ks[5], (C,), jnp.float32) * 0.1
        var2 = jax.random.uniform(ks[6], (C,), jnp.float32, 0.5, 1.5)
        return dict(x=x, w1=w1, w2=w2, gamma1=gamma1, beta1=beta1, mean1=mean1, var1=var1, gamma2=gamma2, beta2=beta2, mean2=mean2, var2=var2)
    _L1_conv_all = _L1_conv_setup()
    _L1_conv_in = {k: v for k, v in _L1_conv_all.items() if k in ('w1', 'w2', 'gamma1', 'beta1', 'mean1', 'var1', 'gamma2', 'beta2', 'mean2', 'var2', )}
    del _L1_conv_all

    def _L2_attn_setup():
        import jax, jax.numpy as jnp
        import numpy as np
        key = jax.random.key(seed)
        k1, k2, k3 = jax.random.split(key, 3)
        B = jax.random.normal(k1, (4, 512, 128), dtype=jnp.float32)
        W = jax.random.normal(k2, (128, 128), dtype=jnp.float32) * (1.0 / np.sqrt(128))
        v = jax.random.uniform(k3, (128,), dtype=jnp.float32)
        return {'B': B, 'W': W, 'v': v}
    _L2_attn_all = _L2_attn_setup()
    _L2_attn_in = {k: v for k, v in _L2_attn_all.items() if k in ('W', 'v', )}
    del _L2_attn_all

    def _L2_ffn_setup():
        import jax, jax.numpy as jnp
        import numpy as np
        B, N, D, C, E, K = (8, 8192, 128, 128, 8, 2)
        key = jax.random.key(seed)
        k0, k1, k2 = jax.random.split(key, 3)
        x = jax.random.normal(k0, (B, N, D), dtype=jnp.float32)
        router_w = jax.random.normal(k1, (D, E), dtype=jnp.float32) * 0.05
        router_b = jnp.zeros((E,), dtype=jnp.float32)
        expert_w = jax.random.normal(k2, (E, D, C), dtype=jnp.float32) * (1.0 / np.sqrt(D))
        expert_b = jnp.zeros((E, C), dtype=jnp.float32)
        return {'x': x, 'router_w': router_w, 'router_b': router_b, 'expert_w': expert_w, 'expert_b': expert_b}
    _L2_ffn_all = _L2_ffn_setup()
    _L2_ffn_in = {k: v for k, v in _L2_ffn_all.items() if k in ('router_w', 'router_b', 'expert_w', 'expert_b', )}
    del _L2_ffn_all

    def _L3_attn_setup():
        import jax, jax.numpy as jnp
        import numpy as np
        B, T, D = (4, 2048, 128)
        key = jax.random.key(seed)
        k1, k2, k3 = jax.random.split(key, 3)
        x = jax.random.normal(k1, (B, T, D), dtype=jnp.float32)
        lim = 1.0 / np.sqrt(D)
        W = jax.random.uniform(k2, (3 * D, D), dtype=jnp.float32, minval=-lim, maxval=lim)
        b = jax.random.uniform(k3, (3 * D,), dtype=jnp.float32, minval=-lim, maxval=lim)
        return {'x': x, 'W': W, 'b': b}
    _L3_attn_all = _L3_attn_setup()
    _L3_attn_in = {k: v for k, v in _L3_attn_all.items() if k in ('W', 'b', )}
    del _L3_attn_all

    def _L3_ffn_setup():
        import jax, jax.numpy as jnp
        import numpy as np
        PADDED_SL = 8192
        TEMPERATURE = 1.0
        SIGMA_POW = 0.25

        def _stu_conv(phi, u, n):
            b, sl, d = u.shape
            sgn = jnp.where(jnp.arange(sl) % 2 == 0, 1.0, -1.0).astype(u.dtype)
            sgn3 = sgn[None, :, None]
            Vf = jnp.fft.rfft(phi, n=n, axis=0)
            Uf_p = jnp.fft.rfft(u, n=n, axis=1)
            Uf_m = jnp.fft.rfft(u * sgn3, n=n, axis=1)
            U_plus = jnp.fft.irfft(Vf[None, :, :, None] * Uf_p[:, :, None, :], n=n, axis=1)[:, :sl]
            U_minus = jnp.fft.irfft(Vf[None, :, :, None] * Uf_m[:, :, None, :], n=n, axis=1)[:, :sl]
            U_minus = U_minus * sgn[None, :, None, None]
            return (U_plus, U_minus)

        def _compute_spectral(u, sigma, phi, Mpp, Mpm):
            U_plus, U_minus = _stu_conv(phi, u, PADDED_SL)
            s = sigma ** SIGMA_POW
            out = jnp.einsum('btkd,k,kde->bte', U_plus, s, Mpp)
            out = out + jnp.einsum('btkd,k,kde->bte', U_minus, s, Mpm)
            return out

        def _compute_ar_u(Mu, u):
            sl = u.shape[1]
            out = jnp.zeros(u.shape[:2] + (Mu.shape[-1],), dtype=u.dtype)
            for i in range(Mu.shape[0]):
                ui = jnp.pad(u, ((0, 0), (i, 0), (0, 0)))[:, :sl]
                out = out + jnp.einsum('btd,de->bte', ui, Mu[i])
            return out

        def _stu(u, sigma, phi, Mu, Mpp, Mpm):
            return _compute_spectral(u, sigma, phi, Mpp, Mpm) + _compute_ar_u(Mu, u)
        key = jax.random.key(seed)
        ks = jax.random.split(key, 8)
        b, sl, d, K, k_u = (2, 4096, 128, 16, 3)
        x = jax.random.normal(ks[0], (b, sl, d), dtype=jnp.float32)
        sigma = jax.random.uniform(ks[1], (K,), dtype=jnp.float32, minval=0.001, maxval=1.0)
        phi = jax.random.normal(ks[2], (sl, K), dtype=jnp.float32) / np.sqrt(sl)
        M_u = jax.random.normal(ks[3], (4, k_u, d, d), dtype=jnp.float32) * 0.02
        M_phi_plus = jax.random.normal(ks[4], (4, K, d, d), dtype=jnp.float32) * 0.02
        M_phi_minus = jax.random.normal(ks[5], (4, K, d, d), dtype=jnp.float32) * 0.02
        log_weights = jnp.ones((4,), dtype=jnp.float32)
        u01 = jax.random.uniform(ks[6], (4,), dtype=jnp.float32, minval=1e-06, maxval=1.0 - 1e-06)
        gumbel = -jnp.log(-jnp.log(u01))
        return {'x': x, 'sigma': sigma, 'phi': phi, 'M_u': M_u, 'M_phi_plus': M_phi_plus, 'M_phi_minus': M_phi_minus, 'log_weights': log_weights, 'gumbel': gumbel}
    _L3_ffn_all = _L3_ffn_setup()
    _L3_ffn_in = {k: v for k, v in _L3_ffn_all.items() if k in ('sigma', 'phi', 'M_u', 'M_phi_plus', 'M_phi_minus', 'log_weights', 'gumbel', )}
    del _L3_ffn_all

    return {
        "x": x,
        "L0_conv_W": _L0_conv_in["W"],
        "L1_conv_w1": _L1_conv_in["w1"],
        "L1_conv_w2": _L1_conv_in["w2"],
        "L1_conv_gamma1": _L1_conv_in["gamma1"],
        "L1_conv_beta1": _L1_conv_in["beta1"],
        "L1_conv_mean1": _L1_conv_in["mean1"],
        "L1_conv_var1": _L1_conv_in["var1"],
        "L1_conv_gamma2": _L1_conv_in["gamma2"],
        "L1_conv_beta2": _L1_conv_in["beta2"],
        "L1_conv_mean2": _L1_conv_in["mean2"],
        "L1_conv_var2": _L1_conv_in["var2"],
        "L2_attn_W": _L2_attn_in["W"],
        "L2_attn_v": _L2_attn_in["v"],
        "L2_ffn_router_w": _L2_ffn_in["router_w"],
        "L2_ffn_router_b": _L2_ffn_in["router_b"],
        "L2_ffn_expert_w": _L2_ffn_in["expert_w"],
        "L2_ffn_expert_b": _L2_ffn_in["expert_b"],
        "L3_attn_W": _L3_attn_in["W"],
        "L3_attn_b": _L3_attn_in["b"],
        "L3_ffn_sigma": _L3_ffn_in["sigma"],
        "L3_ffn_phi": _L3_ffn_in["phi"],
        "L3_ffn_M_u": _L3_ffn_in["M_u"],
        "L3_ffn_M_phi_plus": _L3_ffn_in["M_phi_plus"],
        "L3_ffn_M_phi_minus": _L3_ffn_in["M_phi_minus"],
        "L3_ffn_log_weights": _L3_ffn_in["log_weights"],
        "L3_ffn_gumbel": _L3_ffn_in["gumbel"],
    }

def reference(x, L0_conv_W, L1_conv_w1, L1_conv_w2, L1_conv_gamma1, L1_conv_beta1, L1_conv_mean1, L1_conv_var1, L1_conv_gamma2, L1_conv_beta2, L1_conv_mean2, L1_conv_var2, L2_attn_W, L2_attn_v, L2_ffn_router_w, L2_ffn_router_b, L2_ffn_expert_w, L2_ffn_expert_b, L3_attn_W, L3_attn_b, L3_ffn_sigma, L3_ffn_phi, L3_ffn_M_u, L3_ffn_M_phi_plus, L3_ffn_M_phi_minus, L3_ffn_log_weights, L3_ffn_gumbel):
    import jax
    import jax.numpy as jnp
    def _L0_conv_ref(x, W):
        import jax, jax.numpy as jnp
        import numpy as np
        B, C, H, W_SP = (16, 128, 28, 28)
        F, KS, STRIDE, PAD = (128, 3, 1, 1)
        CHUNK = 4
        EPS = 1e-12

        def _patches(x):
            p = jax.lax.conv_general_dilated_patches(x, (KS, KS), (STRIDE, STRIDE), [(PAD, PAD), (PAD, PAD)], dimension_numbers=('NCHW', 'OIHW', 'NCHW'))
            b, k, ho, wo = p.shape
            return (p.reshape(b, k, ho * wo), ho, wo)
        P, ho, wo = _patches(x)
        Wc = W.reshape(F, -1)
        K = Wc.shape[1]
        Wch = Wc.reshape(F // CHUNK, CHUNK, K)

        def chunk_fn(wc):
            return jnp.sum(jnp.abs(wc[None, :, :, None] - P[:, None, :, :]), axis=2)
        neg_l1 = -jax.lax.map(chunk_fn, Wch)
        neg_l1 = jnp.transpose(neg_l1, (1, 0, 2, 3)).reshape(P.shape[0], F, -1)
        d2 = jnp.sum(Wc * Wc, axis=1)[None, :, None] + jnp.sum(P * P, axis=1)[:, None, :] - 2.0 * jnp.einsum('fk,bkl->bfl', Wc, P)
        neg_l2 = -jnp.sqrt(jnp.maximum(d2, EPS))
        out = neg_l2 + jax.lax.stop_gradient(neg_l1 - neg_l2)
        return out.reshape(P.shape[0], F, ho, wo)

    def _L1_conv_ref(x, w1, w2, gamma1, beta1, mean1, var1, gamma2, beta2, mean2, var2):
        import jax, jax.numpy as jnp
        import numpy as np
        A_BIT = 4
        W_BIT = 4
        EPS = 1e-05
        L_TH = 2

        def _pattern_mask():
            m = np.ones((3, 3), np.float32)
            m[0, 0] = 0.0
            m[2, 2] = 0.0
            return jnp.asarray(m)

        def ste_round(x):
            return x + jax.lax.stop_gradient(jnp.round(x) - x)

        def qfn(x, k):
            n = float(2 ** k - 1)
            return ste_round(x * n) / n

        def act_quant(x, k):
            return qfn(jnp.clip(x, 0.0, 1.0), k)

        def weight_quant(w, k):
            t = jnp.tanh(w)
            t = t / (2.0 * jnp.max(jnp.abs(t))) + 0.5
            return 2.0 * qfn(t, k) - 1.0

        def bn_eval(x, gamma, beta, mean, var):
            inv = gamma / jnp.sqrt(var + EPS)
            return x * inv[None, :, None, None] + (beta - mean * inv)[None, :, None, None]

        def conv3x3(x, w):
            return jax.lax.conv_general_dilated(x, w, window_strides=(1, 1), padding=[(1, 1), (1, 1)], dimension_numbers=('NCHW', 'OIHW', 'NCHW'))
        mask = _pattern_mask()
        wq1 = weight_quant(w1, W_BIT) * mask
        out = act_quant(bn_eval(conv3x3(x, wq1), gamma1, beta1, mean1, var1), A_BIT)
        wq2 = weight_quant(w2, W_BIT) * mask
        out = bn_eval(conv3x3(out, wq2), gamma2, beta2, mean2, var2)
        out = out + x
        return act_quant(out, A_BIT)

    def _L2_attn_ref(B, W, v):
        import jax, jax.numpy as jnp
        import numpy as np
        Wi = jnp.einsum('bnd,ed->bne', B, W)
        scores = jnp.einsum('d,bijd->bij', v, jnp.tanh(Wi[:, None, :, :] + Wi[:, :, None, :]))
        attn = jax.nn.softmax(scores, axis=-1)
        C = jnp.einsum('bij,bjd->bid', attn, B)
        return C

    def _L2_ffn_ref(x, router_w, router_b, expert_w, expert_b):
        import jax, jax.numpy as jnp
        import numpy as np
        B, N, D, C, E, K = (8, 8192, 128, 128, 8, 2)
        router_probs = jax.nn.softmax(x @ router_w + router_b, axis=-1)
        top_p, top_i = jax.lax.top_k(router_probs, K)
        top_p = top_p / jnp.sum(top_p, axis=-1, keepdims=True)
        expert_out = jnp.einsum('bnd,edc->bnec', x, expert_w) + expert_b
        gathered = jnp.take_along_axis(expert_out, top_i[..., None], axis=2)
        return jnp.einsum('bnk,bnkc->bnc', top_p, gathered)

    def _L3_attn_ref(x, W, b):
        import jax, jax.numpy as jnp
        import numpy as np
        B, T, D = (4, 2048, 128)
        Bx, Tx, Dx = x.shape
        qkv = (x @ W.T + b).reshape(Bx, Tx, 3, Dx)
        q, k, v = (qkv[:, :, 0], qkv[:, :, 1], qkv[:, :, 2])
        q = jax.nn.elu(q) + 1.0
        k = jax.nn.elu(k) + 1.0
        kv = jnp.einsum('bti,btj->btij', k, v)
        kv_cum = jnp.cumsum(kv, axis=1)
        k_cum = jnp.cumsum(k, axis=1)
        num = jnp.einsum('bti,btij->btj', q, kv_cum)
        den = jnp.einsum('bti,bti->bt', q, k_cum)[..., None] + 1e-06
        return num / den

    def _L3_ffn_ref(x, sigma, phi, M_u, M_phi_plus, M_phi_minus, log_weights, gumbel):
        import jax, jax.numpy as jnp
        import numpy as np
        PADDED_SL = 8192
        TEMPERATURE = 1.0
        SIGMA_POW = 0.25

        def _stu_conv(phi, u, n):
            b, sl, d = u.shape
            sgn = jnp.where(jnp.arange(sl) % 2 == 0, 1.0, -1.0).astype(u.dtype)
            sgn3 = sgn[None, :, None]
            Vf = jnp.fft.rfft(phi, n=n, axis=0)
            Uf_p = jnp.fft.rfft(u, n=n, axis=1)
            Uf_m = jnp.fft.rfft(u * sgn3, n=n, axis=1)
            U_plus = jnp.fft.irfft(Vf[None, :, :, None] * Uf_p[:, :, None, :], n=n, axis=1)[:, :sl]
            U_minus = jnp.fft.irfft(Vf[None, :, :, None] * Uf_m[:, :, None, :], n=n, axis=1)[:, :sl]
            U_minus = U_minus * sgn[None, :, None, None]
            return (U_plus, U_minus)

        def _compute_spectral(u, sigma, phi, Mpp, Mpm):
            U_plus, U_minus = _stu_conv(phi, u, PADDED_SL)
            s = sigma ** SIGMA_POW
            out = jnp.einsum('btkd,k,kde->bte', U_plus, s, Mpp)
            out = out + jnp.einsum('btkd,k,kde->bte', U_minus, s, Mpm)
            return out

        def _compute_ar_u(Mu, u):
            sl = u.shape[1]
            out = jnp.zeros(u.shape[:2] + (Mu.shape[-1],), dtype=u.dtype)
            for i in range(Mu.shape[0]):
                ui = jnp.pad(u, ((0, 0), (i, 0), (0, 0)))[:, :sl]
                out = out + jnp.einsum('btd,de->bte', ui, Mu[i])
            return out

        def _stu(u, sigma, phi, Mu, Mpp, Mpm):
            return _compute_spectral(u, sigma, phi, Mpp, Mpm) + _compute_ar_u(Mu, u)
        T = x.shape[1]
        outs = []
        for i, frac in enumerate((1, 2, 4, 8)):
            xi = x[:, :T // frac]
            si = _stu(xi, sigma, phi, M_u[i], M_phi_plus[i], M_phi_minus[i])
            si = jnp.pad(si, ((0, 0), (0, T - si.shape[1]), (0, 0)))
            outs.append(si)
        y_soft = jax.nn.softmax((log_weights + gumbel) / TEMPERATURE)
        y_hard = jax.nn.one_hot(jnp.argmax(y_soft), 4, dtype=y_soft.dtype)
        weights = y_hard - jax.lax.stop_gradient(y_soft) + y_soft
        stacked = jnp.stack(outs, axis=-1)
        return jnp.sum(stacked * weights, axis=-1)

    def _gn(v, G=32, eps=1e-5):
        B_, C_, H_, W_ = v.shape
        g = v.reshape(B_, G, C_ // G, H_, W_)
        m = jnp.mean(g, axis=(2, 3, 4), keepdims=True)
        s = jnp.var(g, axis=(2, 3, 4), keepdims=True)
        return ((g - m) / jnp.sqrt(s + eps)).reshape(v.shape)

    def _ln_c(v, eps=1e-6):
        m = jnp.mean(v, axis=1, keepdims=True)
        s = jnp.var(v, axis=1, keepdims=True)
        return (v - m) / jnp.sqrt(s + eps)

    def _ln_t(v, eps=1e-5):
        m = jnp.mean(v, axis=-1, keepdims=True)
        s = jnp.var(v, axis=-1, keepdims=True)
        return (v - m) / jnp.sqrt(s + eps)

    def _to_tokens(v):
        B_, C_, H_, W_ = v.shape
        return v.reshape(B_, C_, H_ * W_).transpose(0, 2, 1)
    def _from_tokens(t, like):
        B_, C_, H_, W_ = like.shape
        return t.transpose(0, 2, 1).reshape(B_, C_, H_, W_)

    x = x + _L0_conv_ref(_gn(x), L0_conv_W)
    x = _L1_conv_ref(x, L1_conv_w1, L1_conv_w2, L1_conv_gamma1, L1_conv_beta1, L1_conv_mean1, L1_conv_var1, L1_conv_gamma2, L1_conv_beta2, L1_conv_mean2, L1_conv_var2)
    t = _to_tokens(x)
    t = t + _L2_attn_ref(_ln_t(t), L2_attn_W, L2_attn_v)
    t = t + _L2_ffn_ref(_ln_t(t), L2_ffn_router_w, L2_ffn_router_b, L2_ffn_expert_w, L2_ffn_expert_b)
    t = t + _L3_attn_ref(_ln_t(t), L3_attn_W, L3_attn_b)
    t = t + _L3_ffn_ref(_ln_t(t), L3_ffn_sigma, L3_ffn_phi, L3_ffn_M_u, L3_ffn_M_phi_plus, L3_ffn_M_phi_minus, L3_ffn_log_weights, L3_ffn_gumbel)
    x = _from_tokens(t, x)
    return x


_drawn_inputs = setup_inputs


def setup_inputs(seed=0):
    import zlib

    import numpy as np

    out = dict(_drawn_inputs(seed))
    spreads = {'L1_conv_gamma1': (1.0, 0.2),
     'L1_conv_beta1': (0.0, 0.1),
     'L1_conv_gamma2': (1.0, 0.2),
     'L1_conv_beta2': (0.0, 0.1),
     'L2_ffn_router_b': (0.0, 0.1),
     'L2_ffn_expert_b': (0.0, 0.1),
     'L3_ffn_log_weights': (1.0, 0.2)}
    factors = {}
    for name, (base, spread) in spreads.items():
        noise = np.random.default_rng([zlib.crc32(name.encode()), seed]).standard_normal(out[name].shape)
        drawn = base * np.exp(spread * noise) if base else spread * noise
        out[name] = jnp.asarray(drawn.astype(out[name].dtype))
    for name, factor in factors.items():
        out[name] = (out[name] * factor).astype(out[name].dtype)
    return out
```

```python
from contextlib import ExitStack
import numpy as np
import concourse.bass as bass
from concourse import mybir
F32 = mybir.dt.float32
BF16 = mybir.dt.bfloat16
ALU = mybir.AluOpType
ACT = mybir.ActivationFunctionType
AX = mybir.AxisListType
RMAX = bass.bass_isa.ReduceOp.max

C = 128; HW = 28; T = HW * HW; PW = HW + 2; HALF = T // 2; ROWS = HW // 2
TAPS = 9; RING = 2; ROUND = 1.5 * 2.0 ** 23; LEVELS = 15.0
BN_EPS = 1e-5
KEPT_TAPS = [t for t in range(TAPS) if t not in (0, 8)]
VEC_SHARE = [3 if r % 2 == 0 else 2 for r in range(32)]
VEC_TILES = sum(VEC_SHARE); ACT_TILES = 4 * 32 - VEC_TILES

def conv_layers(nc, ai, x1, NP):
    with ExitStack() as ctx:
        sb = lambda n, s, d=F32: ctx.enter_context(nc.sbuf_tensor("c_" + n, s, d))
        pb = lambda n, s, d=F32: ctx.enter_context(nc.psum_tensor("c_" + n, s, d))
        sem = lambda n: ctx.enter_context(nc.semaphore("c_" + n))
        onehot = sb("onehot", [128, 32, 32])
        group_avg = sb("group_avg", [128, 128])
        minus_half = sb("minus_half", [128, 128])
        zero_bf = sb("zero_bf", [128, 392 + 128], BF16)
        w0 = sb("w0", [128, TAPS, 128]); w0_neg = sb("w0_neg", [128, TAPS, 128]); w0_rows = sb("w0_rows", [128, TAPS * C])
        w0_sum = sb("w0_sum", [128, 1])
        wq1 = sb("wq1", [128, TAPS, 128]); wq2 = sb("wq2", [128, TAPS, 128]); wq2b = sb("wq2b", [128, TAPS, 128], BF16)
        wmax = sb("wmax", [128, 2]); wmax_all = sb("wmax_all", [128, 2]); wscale = sb("wscale", [128, 2])
        bn = sb("bn", [128, 8]); bn_std = sb("bn_std", [128, 2]); bn_scale = sb("bn_scale", [128, 2]); bn_shift = sb("bn_shift", [128, 2]); bn_q = sb("bn_q", [128, 2])
        xin = sb("xin", [128, 2, T])
        xn = sb("xn", [128, 2, PW, PW])
        rows3 = sb("rows3", [128, 2, PW, HW]); box = sb("box", [128, 2, HW, HW])
        ring = sb("ring", [128, RING, 4, 2 * T])
        stats = sb("stats", [128, 2, 2, 6]); mv = sb("mv", [128, 2, 2]); gmv = sb("gmv", [128, 2, 2]); pad = sb("pad", [128, 2])
        dev = sb("dev", [128, 2]); dev2 = sb("dev2", [128, 2]); gvar = sb("gvar", [128, 2]); gstd = sb("gstd", [128, 2]); grstd = sb("grstd", [128, 2])
        act1 = sb("act1", [128, 4, HALF]); actq = sb("actq", [128, 4, HALF]); xq = sb("xq", [128, 2, PW, PW], BF16)
        tmp = sb("tmp", [128, 4, HALF]); xout = sb("xout", [128, 2, T])
        acc = pb("acc", [128, 4, 512]); psg = pb("psg", [128, 512])

        s_ld = sem("weights_loaded"); s_const = sem("constants_ready"); s_vs = sem("vec_setup"); s_tanh = sem("tanh_ready"); s_mxa = sem("max_all_ready")
        s_x = sem("x_loaded"); s_xfree = sem("x_free"); s_stat = sem("stats_ready"); s_gmean = sem("group_mean_ready"); s_dev = sem("dev_ready")
        s_gdev = sem("group_dev_ready"); s_gvar = sem("group_var_ready"); s_gstd = sem("group_std_ready"); s_xn = sem("xn_ready")
        s_box = sem("box_ready"); s_pool = sem("pool_chain"); s_tv = sem("tiles_vec"); s_ta = sem("tiles_act"); s_free = sem("ring_free")
        s_acc = sem("distance_ready"); s_x1 = sem("x1_ready"); s_v = sem("vec_chain")
        s_c1 = sem("conv1_ready"); s_a1 = sem("act1_ready"); s_q = sem("quant_ready"); s_c2 = sem("conv2_ready"); s_o = sem("xout_ready"); s_st = sem("x1_stored")
        s_bstd = sem("bn_std_ready"); s_wact = sem("weights_act_neg")
        s_accr = sem("acc_read")
        block = ctx.enter_context(nc.Block())

        @block.sync
        def _(sp):
            sp.dma_start(w0[:, :, :], ai["w0t"]).then_inc(s_ld, 16)
            sp.dma_start(w0_rows[:, :], ai["w0r"]).then_inc(s_st, 16)
            sp.dma_start(wq1[:, :, :], ai["w1t"]).then_inc(s_ld, 16)
            sp.dma_start(wq2[:, :, :], ai["w2t"]).then_inc(s_ld, 16)
            for n, k in enumerate(["gamma1", "gamma2", "beta1", "beta2", "mean1", "mean2", "var1", "var2"]):
                sp.dma_start(bn[:, n:n + 1], ai[k].rearrange("(c o) -> c o", o=1)).then_inc(s_ld, 16)
            sp.dma_start(xin[:, :, :], ai["x"][0:1].rearrange("a i c t -> c (a i) t")).then_inc(s_x, 16)
            with sp.Fori(0, NP - 1) as p:
                sp.wait_ge(s_x1, p + 1)
                sp.dma_start(xin[:, :, :], ai["x"][bass.ds(p + 1, 1)].rearrange("a i c t -> c (a i) t")).then_inc(s_x, 16)
                sp.wait_ge(s_o, 4 * p + 4)
                sp.dma_start(x1[bass.ds(p, 1)].rearrange("a i c t -> c (a i) t"), xout[:, :, :]).then_inc(s_st, 16)
            sp.wait_ge(s_o, 4 * NP)
            sp.dma_start(x1[NP - 1:NP].rearrange("a i c t -> c (a i) t"), xout[:, :, :]).then_inc(s_st, 16)
            sp.wait_ge(s_st, 16 * NP + 16)

        @block.gpsimd
        def _(pool):
            pool.memset(onehot[:, :, :], 0.0).then_inc(s_pool, 1)
            pool.memset(group_avg[:, :], 0.25).then_inc(s_pool, 1)
            pool.memset(minus_half[:, :], -0.5).then_inc(s_pool, 1)
            pool.memset(zero_bf[:, :], 0.0).then_inc(s_pool, 1)
            pool.memset(pad[:, 1:2], 0.0).then_inc(s_accr, 4)
            pool.memset(xn[:, :, :, :], 0.0).then_inc(s_pool, 1)
            pool.memset(xq[:, :, :, :], 0.0).then_inc(s_pool, 1)
            pool.wait_ge(s_pool, 6)
            pool.affine_select(out=onehot[:, :, :], in_=onehot[:, :, :], compare_op=ALU.not_equal, fill=1.0, base=0, pattern=[[1, 32], [-1, 32]], channel_multiplier=0).then_inc(s_pool, 1)
            g3 = group_avg[:, :].rearrange("p (g k) -> p g k", k=4)
            pool.affine_select(out=g3, in_=g3, compare_op=ALU.is_ge, fill=0.0, base=0, pattern=[[-4, 32], [0, 4]], channel_multiplier=1).then_inc(s_pool, 1)
            pool.wait_ge(s_pool, 8)
            pool.affine_select(out=g3, in_=g3, compare_op=ALU.is_ge, fill=0.0, base=3, pattern=[[4, 32], [0, 4]], channel_multiplier=-1).then_inc(s_pool, 1)
            pool.wait_ge(s_pool, 9)
            pool.wait_ge(s_vs, 2)
            pool.partition_all_reduce(wmax_all[:, :], wmax[:, :], 128, RMAX).then_inc(s_mxa, 1)
            with pool.Fori(0, NP) as p:
                pool.wait_ge(s_xn, 2 * p + 2)
                k = 9
                K = 3
                def link(ins, n):
                    ins.then_inc(s_pool, 1)
                    pool.wait_ge(s_pool, K * p + 9 + n)
                link(pool.tensor_tensor(rows3[:, :, :, :], xn[:, :, :, 0:HW], xn[:, :, :, 1:1 + HW], ALU.add), 1)
                link(pool.tensor_tensor(rows3[:, :, :, :], rows3[:, :, :, :], xn[:, :, :, 2:2 + HW], ALU.add), 2)
                link(pool.tensor_tensor(box[:, :, :, :], rows3[:, :, 0:HW, :], rows3[:, :, 1:1 + HW, :], ALU.add), 3)
                pool.tensor_tensor(box[:, :, :, :], box[:, :, :, :], rows3[:, :, 2:2 + HW, :], ALU.add).then_inc(s_box, 1)

        @block.tensor
        def _(pe):
            pe.wait_ge(s_pool, 9)
            pe.matmul(psg[:, 0:4], group_avg[:, :], minus_half[:, 0:4], start=True, stop=True).then_inc(s_free, RING)
            with pe.Fori(0, NP) as p:
                pe.wait_ge(s_stat, 2 * p + 2)
                pe.matmul(psg[:, 0:4], group_avg[:, :], mv[:, :, :], start=True, stop=True).then_inc(s_gmean, 1)
                pe.wait_ge(s_dev, p + 1)
                pe.matmul(psg[:, 8:10], group_avg[:, :], dev2[:, :], start=True, stop=True).then_inc(s_gdev, 1)
                pe.wait_ge(s_accr, 4 * p + 4)
                for ch in range(4):
                    pe.matmul(acc[:, ch, 0:HALF], zero_bf[:, 0:128], zero_bf[:, 128:128 + HALF], start=True, stop=False, skip_group_check=True)
                with pe.Fori(0, 3) as dy:
                    with pe.Fori(0, 3) as dx:
                        j = 9 * p + 3 * dy + dx
                        vec = act = 0
                        for r in range(32):
                            vec += VEC_SHARE[r]; act += 4 - VEC_SHARE[r]
                            pe.wait_ge(s_tv, j * VEC_TILES + vec)
                            pe.wait_ge(s_ta, j * ACT_TILES + act)
                            for ch in range(4):
                                for g in range(4):
                                    mm = pe.matmul(acc[32 * g:32 * g + 32, ch, 0:HALF], onehot[:, r, :], ring[:, r % RING, g, ch * HALF:(ch + 1) * HALF],
                                                   start=False, stop=False, skip_group_check=True)
                            mm.then_inc(s_free, 1)
                pe.wait_ge(s_box, p + 1)
                bx = box[:, :, :, :].rearrange("c i h w -> c (i h w)")
                for ch in range(4):
                    mm = pe.matmul(acc[:, ch, 0:HALF], minus_half[:, :], bx[:, ch * HALF:(ch + 1) * HALF], start=False, stop=True, skip_group_check=True)
                mm.then_inc(s_acc, 1)
                pe.wait_ge(s_x1, p + 1)
                for im in range(2):
                    for h in range(2):
                        for t in KEPT_TAPS:
                            y, x = t // 3, t % 3
                            mm = pe.matmul(acc[:, 2 * im + h, 0:HALF], wq1[:, t, :], xn[:, im, y + ROWS * h:y + ROWS * (h + 1), x:x + HW],
                                           start=(t == KEPT_TAPS[0]), stop=(t == KEPT_TAPS[-1]))
                        mm.then_inc(s_c1, 1)
                for im in range(2):
                    pe.wait_ge(s_q, 4 * p + 2 * im + 2)
                    for h in range(2):
                        for t in KEPT_TAPS:
                            y, x = t // 3, t % 3
                            mm = pe.matmul(acc[:, 2 * im + h, 0:HALF], wq2b[:, t, :], xq[:, im, y + ROWS * h:y + ROWS * (h + 1), x:x + HW],
                                           start=(t == KEPT_TAPS[0]), stop=(t == KEPT_TAPS[-1]))
                        mm.then_inc(s_c2, 1)

        @block.scalar
        def _(act):
            act.wait_ge(s_ld, 16 * 11)
            act.activation(wq1[:, :, :], wq1[:, :, :], ACT.Tanh).then_inc(s_tanh, 1)
            act.activation(wq2[:, :, :], wq2[:, :, :], ACT.Tanh).then_inc(s_tanh, 1)
            act.activation(w0_neg[:, :, :], w0[:, :, :], ACT.Copy, scale=-1.0).then_inc(s_wact, 1)
            act.wait_ge(s_vs, 3)
            act.activation(bn_std[:, :], bn[:, 6:8], ACT.Sqrt).then_inc(s_bstd, 1)
            act.wait_ge(s_wact, 1)
            with act.Fori(0, NP) as p:
                act.wait_ge(s_gvar, p + 1)
                act.activation(gstd[:, :], gvar[:, :], ACT.Sqrt).then_inc(s_gstd, 1)
                act.wait_ge(s_xn, 2 * p + 2)
                with act.Fori(0, 3) as dy:
                    with act.Fori(0, 3) as dx:
                        j = 9 * p + 3 * dy + dx
                        for r in range(32):
                            act.wait_ge(s_free, j * 32 + r + 1)
                            for g in range(VEC_SHARE[r], 4):
                                act.activation(ring[:, r % RING, g, :].rearrange("c (i h w) -> c i h w", i=2, h=HW), xn[:, :, bass.ds(dy, HW), bass.ds(dx, HW)], ACT.Relu,
                                               bias=w0_neg[:, bass.ds(3 * dy + dx, 1), 4 * r + g]).then_inc(s_ta, 1)
                for c in range(4):
                    act.wait_ge(s_c1, 4 * p + c + 1)
                    act.activation(act1[:, c, :], acc[:, c, 0:HALF], ACT.Relu, scale=bn_q[:, 0:1], bias=bn_shift[:, 0:1]).then_inc(s_a1, 1)

        @block.vector
        def _(dve):
            n = [0]
            def link(ins):
                n[0] += 1
                ins.then_inc(s_v, 1)
                dve.wait_ge(s_v, n[0])
            dve.wait_ge(s_tanh, 2)
            dve.wait_ge(s_st, 16)
            for q, wq in enumerate((wq1, wq2)):
                dve.tensor_reduce(wmax[:, q:q + 1], wq[:, :, :], AX.XY, ALU.max, apply_absolute_value=True).then_inc(s_vs, 1)
            link(dve.tensor_scalar(bn[:, 6:8], bn[:, 6:8], BN_EPS, None, ALU.add))
            dve.tensor_reduce(w0_sum[:, :], w0_rows[:, :], AX.X, ALU.add).then_inc(s_vs, 1)
            dve.wait_ge(s_vs, 3)
            dve.wait_ge(s_mxa, 1)
            link(dve.tensor_scalar(wmax_all[:, :], wmax_all[:, :], 2.0, None, ALU.mult))
            link(dve.reciprocal(wscale[:, :], wmax_all[:, :]))
            for q, wq in enumerate((wq1, wq2)):
                link(dve.tensor_scalar(wq[:, :, :], wq[:, :, :], wscale[:, q:q + 1], 0.5, ALU.mult, ALU.add))
                link(dve.tensor_scalar(wq[:, :, :], wq[:, :, :], LEVELS, ROUND, ALU.mult, ALU.add))
                link(dve.tensor_scalar(wq[:, :, :], wq[:, :, :], ROUND, 2.0, ALU.subtract, ALU.mult))
                link(dve.tensor_scalar((wq1, wq2b)[q][:, :, :], wq[:, :, :], LEVELS, None, ALU.subtract))
            dve.wait_ge(s_bstd, 1)
            link(dve.reciprocal(bn_std[:, :], bn_std[:, :]))
            link(dve.tensor_tensor(bn_scale[:, :], bn[:, 0:2], bn_std[:, :], ALU.mult))
            link(dve.tensor_tensor(bn_shift[:, :], bn[:, 4:6], bn_scale[:, :], ALU.mult))
            link(dve.tensor_tensor(bn_shift[:, :], bn[:, 2:4], bn_shift[:, :], ALU.subtract))
            link(dve.tensor_scalar(bn_q[:, 0:1], bn_scale[:, 0:1], 1.0 / LEVELS, None, ALU.mult))
            link(dve.tensor_scalar(bn_q[:, 1:2], bn_scale[:, 1:2], 1.0 / LEVELS ** 2, None, ALU.mult))
            dve.wait_ge(s_pool, 9)
            dve.wait_ge(s_accr, 4)
            base = n[0]
            K = 28
            with dve.Fori(0, NP) as p:
                n = [0]
                def link(ins):
                    n[0] += 1
                    ins.then_inc(s_v, 1)
                    dve.wait_ge(s_v, K * p + base + n[0])
                dve.wait_ge(s_x, 16 * p + 16)
                for im in range(2):
                    for h in range(2):
                        link(dve.bn_stats(stats[:, im, h, :], xin[:, im, h * HALF:(h + 1) * HALF]))
                n[0] += 1; dve.memset(pad[:, 0:1], 0.0).then_inc(s_v, 1)
                for im in range(2):
                    dve.bn_aggr(mv[:, im, :], stats[:, im, :, :]).then_inc(s_stat, 1)
                dve.wait_ge(s_gmean, p + 1)
                link(dve.tensor_copy(gmv[:, :, :], psg[:, 0:4].rearrange("c (i k) -> c i k", i=2)))
                dve.wait_ge(s_stat, 2 * p + 2)
                link(dve.tensor_tensor(dev[:, :], mv[:, :, 0], gmv[:, :, 0], ALU.subtract))
                dve.tensor_tensor(dev2[:, :], dev[:, :], dev[:, :], ALU.mult).then_inc(s_dev, 1)
                dve.wait_ge(s_gdev, p + 1)
                link(dve.tensor_tensor(gvar[:, :], gmv[:, :, 1], psg[:, 8:10], ALU.add))
                dve.tensor_scalar(gvar[:, :], gvar[:, :], 1e-5, None, ALU.add).then_inc(s_gvar, 1)
                dve.wait_ge(s_gstd, p + 1)
                link(dve.reciprocal(grstd[:, :], gstd[:, :]))
                for im in range(2):
                    dve.tensor_scalar(xn[:, im, 1:1 + HW, 1:1 + HW], xin[:, im, :].rearrange("c (h w) -> c h w", h=HW), gmv[:, im, 0:1], grstd[:, im:im + 1], ALU.subtract, ALU.mult).then_inc(s_xn, 1)
                dve.wait_ge(s_xn, 2 * p + 2)
                n[0] += 1; dve.memset(pad[:, 0:1], 0.0).then_inc(s_v, 1)
                with dve.Fori(0, 3) as dy:
                    with dve.Fori(0, 3) as dx:
                        j = 9 * p + 3 * dy + dx
                        for r in range(32):
                            dve.wait_ge(s_free, j * 32 + r + 1)
                            for g in range(VEC_SHARE[r]):
                                dve.tensor_scalar(ring[:, r % RING, g, :].rearrange("c (i h w) -> c i h w", i=2, h=HW), xn[:, :, bass.ds(dy, HW), bass.ds(dx, HW)],
                                                  w0[:, bass.ds(3 * dy + dx, 1), 4 * r + g], 0.0, ALU.subtract, ALU.max).then_inc(s_tv, 1)
                dve.wait_ge(s_acc, p + 1)
                dve.wait_ge(s_box, p + 1)
                link(dve.tensor_scalar(tmp[:, :, :], acc[:, :, 0:HALF], -2.0, w0_sum[:, 0:1], ALU.mult, ALU.subtract))
                for im in range(2):
                    ins = dve.tensor_tensor(xn[:, im, 1:1 + HW, 1:1 + HW], xin[:, im, :].rearrange("c (h w) -> c h w", h=HW),
                                      tmp[:, 2 * im:2 * im + 2, :].rearrange("c a (h w) -> c (a h) w", w=HW), ALU.add)
                    if im == 0: link(ins)
                ins.then_inc(s_x1, 1)
                dve.wait_ge(s_x1, p + 1)
                for c in range(4):
                    im, h = c // 2, c % 2
                    dve.wait_ge(s_a1, 4 * p + c + 1)
                    link(dve.tensor_scalar(actq[:, c, :], act1[:, c, :], 1.0, LEVELS, ALU.min, ALU.mult))
                    dve.tensor_scalar(xq[:, im, 1 + ROWS * h:1 + ROWS * (h + 1), 1:1 + HW], actq[:, c, :].rearrange("c (h w) -> c h w", w=HW), ROUND, ROUND, ALU.add, ALU.subtract).then_inc(s_q, 1)
                for c in range(4):
                    im, h = c // 2, c % 2
                    dve.wait_ge(s_c2, 4 * p + c + 1)
                    ins = dve.scalar_tensor_tensor(out=tmp[:, c, :].rearrange("c (h w) -> c h w", w=HW), in0=acc[:, c, 0:HALF].rearrange("c (h w) -> c h w", w=HW), scalar=bn_q[:, 1:2],
                                                   in1=xn[:, im, 1 + ROWS * h:1 + ROWS * (h + 1), 1:1 + HW], op0=ALU.mult, op1=ALU.add)
                    ins.then_inc(s_accr, 1)
                    dve.wait_ge(s_accr, 4 * p + c + 5)
                    link(dve.tensor_scalar(tmp[:, c, :], tmp[:, c, :], bn_shift[:, 1:2], 0.0, ALU.add, ALU.max))
                    link(dve.tensor_scalar(tmp[:, c, :], tmp[:, c, :], 1.0, LEVELS, ALU.min, ALU.mult))
                    link(dve.tensor_scalar(tmp[:, c, :], tmp[:, c, :], ROUND, ROUND, ALU.add, ALU.subtract))
                    if c == 0:
                        dve.wait_ge(s_st, 16 * p + 16)
                    dve.tensor_scalar(xout[:, im, h * HALF:(h + 1) * HALF], tmp[:, c, :], 1.0 / LEVELS, None, ALU.mult).then_inc(s_o, 1)
                assert n[0] == K, n[0]

C = 128; T = 784; HALF = 392
NT = 7
TOK_ROWS = [128] * 6 + [16]
TAIL = TOK_ROWS[-1]
STEPS = 32
NB = 2
E8 = 8
NK = 16
SEG = [(196, 392), (98, 196), (49, 98), (0, 49)]
ST = [128, 128, 128, 8]
LN_EPS = 1e-5

def token_layers(nc, ai, x1, out_dram, NI):
    with ExitStack() as ctx:
        sb = lambda n, s, d=F32: ctx.enter_context(nc.sbuf_tensor("t_" + n, s, d))
        pb = lambda n, s, d=F32: ctx.enter_context(nc.psum_tensor("t_" + n, s, d))
        sem = lambda n: ctx.enter_context(nc.semaphore("t_" + n))
        toep = sb("toep", [128, 2 * NK, 393])
        mix = sb("mix", [128, 4, NK, 2, 128])
        mixu = sb("mixu", [128, 4, 3, 128])
        arena = sb("arena", [128, 12700])
        ident = sb("ident", [128, 128]); causal = sb("causal", [128, 128]); vhot = sb("vhot", [128, 32, 32]); vcol = sb("vcol", [128, 1])
        wa = sb("wa", [128, 128]); rw = sb("rw", [128, 8]); rb = sb("rb", [128, 8]); eb = sb("eb", [8, 128]); lower = sb("lower", [128, 8, 8])
        wqkv = sb("wqkv", [128, 384]); bqk = sb("bqk", [128, 2]); bv = sb("bv", [128, 128])
        ew = sb("ew", [128, 1024])
        sg = sb("sg", [128, 16]); lw = sb("lw", [128, 12]); sm8 = sb("sm8", [128, 12]); coef = sb("coef", [128, 4, 16])
        xch = sb("xch", [128, T]); tok = sb("tok", [128, NT, 128]); nrm = sb("nrm", [128, NT, 128]); nrmT = sb("nrmT", [128, T + 2])
        stats = sb("stats", [128, NT, 6]); mv = sb("mv", [128, NT, 2]); var = sb("var", [128, NT]); std = sb("std", [128, NT])
        proj = sb("proj", [128, T])
        small = sb("small", [128, 64]); pad = sb("pad", [128, 8])
        off = [0]
        def carve(shape, parts=128):
            n = int(np.prod(shape)); a = arena[0:parts, off[0]:off[0] + n]; off[0] += n
            assert off[0] <= 12700, off[0]
            if len(shape) == 1: return a
            names = "abcd"[:len(shape)]
            return a.rearrange(f"p ({' '.join(names)}) -> p {' '.join(names)}", **{c: s for c, s in zip(names, shape)})
        mp = carve([NK, 128]); mm_ = carve([NK, 128]); msum = carve([NK, 128]); mdif = carve([NK, 128]); mu = carve([3, 128])
        off[0] = 0
        S = carve([NT, T]); ring = carve([NB, 4, T]); PT = carve([NT, 128])
        off[0] = 0
        logit = carve([NT, 8]); prob = carve([NT, 8]); gt = carve([NT, 8, 8]); eq = carve([NT, 8, 8]); gateT = carve([T], 8)
        zq = carve([T]); zmin = carve([T]); qT = carve([T]); kT = carve([T]); vaug = carve([NT, 129]); AT = carve([sum(T - 128 * i for i in range(NT))])
        res = carve([T]); U = carve([2, 4, 128]); UT = carve([3, HALF])
        ATo = [sum(T - 128 * k for k in range(i)) for i in range(NT)]

        psS = pb("psS", [128, 2, 2, 512]); psA = pb("psA", [128, 1024]); psB = pb("psB", [128, 1024])

        class Ev:
            def __init__(self, name, k, first=0): self.s = sem(name); self.k = k; self.first = first
        s_ld = sem("weights_loaded"); s_br = sem("branch_loaded"); s_brf = sem("branch_used"); s_pc = sem("pool_chain"); s_set = sem("vec_setup"); s_setp = sem("act_setup")
        s_credit = sem("ring_free")
        dch = sem("vec_chain")
        x_in = Ev("x_in", 1); pX = Ev("pX", 1, 1); tT = Ev("tT", 2)
        lnv = Ev("lnv", 4); lns = Ev("lns", 4); lnB = Ev("lnB", 4); pBT = Ev("pBT", 4); eBT = Ev("eBT", 4)
        pWi = Ev("pWi", 1); eWi = Ev("eWi", 1)
        sums = Ev("sums", 6 * STEPS * 4 + 1); th = Ev("th", 6 * STEPS + 1)
        pS = Ev("pS", 7); Sev = Ev("Sev", 7, 1); pF = Ev("pF", 6); eF = Ev("eF", 6); mx = Ev("mx", 7); ex = Ev("ex", 7); eP = Ev("eP", 7); pPT = Ev("pPT", 7); ePT = Ev("ePT", 7)
        pO = Ev("pO", 7); eO = Ev("eO", 7)
        pL = Ev("pL", 1); sub8 = Ev("sub8", 1); exp8 = Ev("exp8", 1); gate = Ev("gate", 1); pGT = Ev("pGT", 1); eGT = Ev("eGT", 1); pY = Ev("pY", 7); eY = Ev("eY", 7)
        pQ = Ev("pQ", 2); zm = Ev("zm", 2); eq_exp = Ev("eqexp", 2); qk = Ev("qk", 2); pV = Ev("pV", 1); eV = Ev("eV", 1)
        pAT = Ev("pAT", 7); eAT = Ev("eAT", 7); pN = Ev("pN", 7); eN = Ev("eN", 7)
        pU = Ev("pU", 2); eU = Ev("eU", 2); pR = Ev("pR", 1); eR = Ev("eR", 1, 1); pC = Ev("pC", 64); eC = Ev("eC", 64); pZ = Ev("pZ", 64 + 2); out_ready = Ev("out_ready", 2)
        stored = Ev("stored", 1)
        block = ctx.enter_context(nc.Block())

        def W(e, ev, k, b):
            e.wait_ge(ev.s, ev.k * b + k + ev.first)

        @block.sync
        def _(sp):
            for dst, src in ((wa[:, :], ai["wa"]), (rw[:, :], ai["rw"]), (eb[:, :], ai["eb"]), (wqkv[:, :], ai["wqkv"]), (ew[:, :], ai["ew"]),
                             (rb[:, :], ai["rb"].partition_broadcast(128)), (bv[:, :], ai["bqkv"][256:384].partition_broadcast(128)),
                             (bqk[:, 0:1], ai["bqkv"][0:128].rearrange("(c o) -> c o", o=1)), (bqk[:, 1:2], ai["bqkv"][128:256].rearrange("(c o) -> c o", o=1)),
                             (vcol[:, :], ai["v"].rearrange("(c o) -> c o", o=1)),
                             (sg[:, :], ai["sigma"].partition_broadcast(128)), (lw[:, 0:4], ai["lw"].partition_broadcast(128)), (lw[:, 4:8], ai["gum"].partition_broadcast(128))):
                sp.dma_start(dst, src).then_inc(s_ld, 16)
            sp.dma_start(toep[:, :, :], ai["toep"]).then_inc(s_ld, 16)
            for i in range(4):
                sp.wait_ge(s_brf, i)
                sp.dma_start(mp, ai["mp"][i].rearrange("k d e -> d k e")).then_inc(s_br, 16)
                sp.dma_start(mm_, ai["mm"][i].rearrange("k d e -> d k e")).then_inc(s_br, 16)
                sp.dma_start(mu, ai["mu"][i].rearrange("k d e -> d k e")).then_inc(s_br, 16)
            with sp.Fori(0, NI) as b:
                W(sp, pX, 0, b)
                sp.dma_start(xch[:, :], x1[bass.ds(b, 1)].rearrange("a c t -> c (a t)")).then_inc(x_in.s, 16)
                W(sp, out_ready, 2, b)
                sp.dma_start(out_dram[bass.ds(b, 1)].rearrange("a c t -> c (a t)"), res).then_inc(stored.s, 16)
            sp.wait_ge(stored.s, 16 * NI)

        @block.gpsimd
        def _(pool):
            for n, ev in enumerate((pX, eR, Sev)):
                pool.memset(pad[:, 2 + n:3 + n], 0.0).then_inc(ev.s, 1)
            pool.memset(ident[:, :], 0.0).then_inc(s_pc, 1)
            pool.memset(causal[:, :], 1.0).then_inc(s_pc, 1)
            pool.memset(vhot[:, :, :], 0.0).then_inc(s_pc, 1)
            pool.memset(lower[:, :, :], 1.0).then_inc(s_pc, 1)
            pool.memset(tok[:, :, :], 0.0).then_inc(s_pc, 1)
            pool.memset(nrmT[:, :], 0.0).then_inc(s_pc, 1)
            pool.wait_ge(s_pc, 6)
            pool.affine_select(out=ident[:, :], in_=ident[:, :], compare_op=ALU.not_equal, fill=1.0, base=0, pattern=[[-1, 128]], channel_multiplier=1).then_inc(s_pc, 1)
            pool.affine_select(out=causal[:, :], in_=causal[:, :], compare_op=ALU.is_ge, fill=0.0, base=0, pattern=[[1, 128]], channel_multiplier=-1).then_inc(s_pc, 1)
            pool.affine_select(out=vhot[:, :, :], in_=vhot[:, :, :], compare_op=ALU.not_equal, fill=1.0, base=0, pattern=[[1, 32], [-1, 32]], channel_multiplier=0).then_inc(s_pc, 1)
            pool.affine_select(out=lower[:, :, :], in_=lower[:, :, :], compare_op=ALU.is_gt, fill=0.0, base=0, pattern=[[1, 8], [-1, 8]], channel_multiplier=0).then_inc(s_pc, 1)

        tiles = range(NT)

        @block.tensor
        def _(pe):
            pe.wait_ge(s_pc, 10)
            pe.wait_ge(s_set, 1)
            pe.matmul(psB[0:32, 0:8], ident[:, 0:32], ident[:, 0:8], start=True, stop=True).then_inc(s_credit, NB)
            with pe.Fori(0, NI) as b:
                def transposes(src_of, dst_of, ev, ns=tiles):
                    for t in ns:
                        ins = pe.transpose(dst_of(t), src_of(t), ident[0:src_of(t).shape[0], 0:src_of(t).shape[0]])
                    ins.then_inc(ev.s, 1)
                def ln(L):
                    W(pe, lnB, L + 1, b)
                    transposes(lambda t: nrm[0:TOK_ROWS[t], t, :], lambda t: psA[:, 128 * t:128 * t + TOK_ROWS[t]], pBT)
                pe.wait_ge(x_in.s, 16 * b + 16)
                W(pe, eR, 0, b)
                transposes(lambda t: xch[:, 128 * t:128 * t + TOK_ROWS[t]], lambda t: psA[0:TOK_ROWS[t], 128 * t:128 * t + 128], pX)
                W(pe, tT, 2, b)
                ln(0)
                W(pe, eBT, 1, b)
                for h in range(2):
                    ins = pe.matmul(psB[:, 512 * h:512 * h + HALF], wa[:, :], nrmT[:, 2 + HALF * h:2 + HALF * (h + 1)], start=True, stop=True)
                ins.then_inc(pWi.s, 1)

                def fill(blk):
                    W(pe, Sev, blk + 1, b)
                    W(pe, ePT, blk, b) if blk else W(pe, eBT, 1, b)
                    transposes(lambda t: S[:, blk, 128 * t:128 * t + TOK_ROWS[t]], lambda t: psA[0:TOK_ROWS[t], 128 * (t - blk - 1):128 * (t - blk)], pF, range(blk + 1, NT))
                def pt(blk):
                    R = TOK_ROWS[blk]
                    if blk < 6:
                        W(pe, eF, min(blk + 1, 6), b)
                        W(pe, eP, blk + 1 if blk < 5 else 7, b)
                    transposes(lambda t: S[0:R, blk, 128 * t:128 * t + TOK_ROWS[t]], lambda t: psA[0:TOK_ROWS[t], 128 * t:128 * t + R], pPT)
                def out(blk):
                    R = TOK_ROWS[blk]
                    W(pe, ePT, blk + 1, b)
                    W(pe, eO, blk, b) if blk else W(pe, eWi, 1, b)
                    for t in tiles:
                        ins = pe.matmul(psB[0:R, 0:128], PT[0:TOK_ROWS[t], t, 0:R], nrm[0:TOK_ROWS[t], t, :], start=(t == 0), stop=(t == 6))
                    ins.then_inc(pO.s, 1)
                for blk in range(NT):
                    W(pe, Sev, max(blk - 1, 0), b)
                    if blk < 6:
                        Wd = T - 128 * blk; nch = 2 if Wd > 512 else 1; w = Wd // nch
                        for r in range(STEPS):
                            st = STEPS * blk + r
                            W(pe, th, st + 1, b)
                            for h in range(nch):
                                for q in range(4):
                                    ins = pe.matmul(psS[32 * q:32 * q + 32, blk % 2, h, 0:w], vhot[:, r, :], ring[:, st % NB, q, h * w:(h + 1) * w],
                                                    start=(r == 0), stop=(r == STEPS - 1), skip_group_check=True)
                            ins.then_inc(s_credit, 1)
                            if blk:
                                if r == 4: fill(blk - 1)
                                if r == 14: pt(blk - 1)
                                if r == 20: out(blk - 1)
                        W(pe, th, STEPS * (blk + 1), b)
                        pe.matmul(psB[0:32, 512:520], ident[:, 0:32], ident[:, 0:8], start=True, stop=True).then_inc(pS.s, 1)
                    else:
                        W(pe, th, 6 * STEPS + 1, b)
                        for r in range(TAIL):
                            ins = pe.matmul(psS[0:32, 0, 0, 0:TAIL], vhot[:, r, :], ring[:, 0, 0, TAIL * r:TAIL * (r + 1)], start=(r == 0), stop=(r == TAIL - 1), skip_group_check=True)
                        ins.then_inc(s_credit, 1)
                        pe.matmul(psB[0:32, 512:520], ident[:, 0:32], ident[:, 0:8], start=True, stop=True).then_inc(pS.s, 1)
                        fill(5); pt(5); out(5)
                        pt(6); out(6)
                ln(1)
                W(pe, eBT, 2, b)
                for t in tiles:
                    ins = pe.matmul(psB[0:TOK_ROWS[t], 512 + 8 * t:520 + 8 * t], nrmT[:, 2 + 128 * t:2 + 128 * t + TOK_ROWS[t]], rw[:, :], start=True, stop=True)
                ins.then_inc(pL.s, 1)
                W(pe, gate, 1, b)
                transposes(lambda t: prob[0:TOK_ROWS[t], t, :], lambda t: psA[0:8, 128 * t:128 * t + TOK_ROWS[t]], pGT)
                W(pe, eGT, 1, b)
                for t in tiles:
                    R = TOK_ROWS[t]
                    if t >= 2: W(pe, eY, t - 1, b)
                    for h in range(2):
                        pe.matmul(psS[0:R, t % 2, h, :], nrmT[:, 2 + 128 * t:2 + 128 * t + R], ew[:, 512 * h:512 * h + 512], start=True, stop=True)
                    ins = pe.matmul(psB[0:R, 512 * (t % 2):512 * (t % 2) + 128], gateT[:, 128 * t:128 * t + R], eb[:, :], start=True, stop=True)
                    ins.then_inc(pY.s, 1)
                ln(2)
                W(pe, eBT, 3, b)
                W(pe, eY, 7, b)
                for a in range(2):
                    for h in range(2):
                        ins = pe.matmul(psS[:, a, h, 0:HALF], wqkv[:, 128 * a:128 * a + 128], nrmT[:, 2 + HALF * h:2 + HALF * (h + 1)], start=True, stop=True)
                    ins.then_inc(pQ.s, 1)
                for t in tiles:
                    ins = pe.matmul(psA[0:TOK_ROWS[t], 128 * t:128 * t + 128], nrmT[:, 2 + 128 * t:2 + 128 * t + TOK_ROWS[t]], wqkv[:, 256:384], start=True, stop=True)
                ins.then_inc(pV.s, 1)
                W(pe, qk, 2, b)
                for i in tiles:
                    Wd = T - 128 * i; nch = 2 if Wd > 512 else 1; w = Wd // nch
                    if i >= 2: W(pe, eAT, i - 1, b)
                    for h in range(nch):
                        ins = pe.matmul(psS[0:TOK_ROWS[i], i % 2, h, 0:w], kT[:, 128 * i:128 * i + TOK_ROWS[i]], qT[:, 128 * i + w * h:128 * i + w * (h + 1)], start=True, stop=True)
                    ins.then_inc(pAT.s, 1)
                W(pe, eV, 1, b)
                for t in tiles:
                    W(pe, eAT, t + 1, b)
                    if t >= 2: W(pe, eN, t - 1, b)
                    R = TOK_ROWS[t]
                    for i in range(t + 1):
                        ins = pe.matmul(psB[0:R, 512 * (t % 2):512 * (t % 2) + 129], AT[0:TOK_ROWS[i], ATo[i] + 128 * (t - i):ATo[i] + 128 * (t - i) + R], vaug[0:TOK_ROWS[i], i, :], start=(i == 0), stop=(i == t))
                    ins.then_inc(pN.s, 1)
                ln(3)
                W(pe, eBT, 4, b)
                for par in range(2):
                    for i in range(4):
                        c0 = 2 + par + 256 * i; n = ST[i]
                        ins = pe.transpose(psA[0:n, 512 * par + 128 * i:512 * par + 128 * i + 128], nrmT[:, c0:c0 + 2 * n - 1:2], ident[:, :])
                    ins.then_inc(pU.s, 1)
                W(pe, eU, 2, b)
                transposes(lambda t: tok[0:TOK_ROWS[t], t, :], lambda t: psA[:, 128 * t:128 * t + TOK_ROWS[t]], pR)
                W(pe, eN, 7, b)
                def conv(n):
                    par, eo, k = n // 32, n // 16 % 2, n % 16
                    if n >= 2: W(pe, eC, n - 1, b)
                    src = par if eo == 0 else 1 - par
                    shift = 1 if (eo == 1 and par == 0) else 0
                    dst = psS[:, n % 2, 0, :]
                    for i in range(4):
                        o = 128 * i; n_ = ST[i]
                        ins = pe.matmul(dst[:, o:HALF], U[0:n_, src, i, :], toep[0:n_, 16 * eo + k, 1 - shift:1 - shift + HALF - o], start=(i == 0), stop=(i == 3), skip_group_check=True)
                    ins.then_inc(pC.s, 1)
                def mixin(n):
                    par, eo, k = n // 32, n // 16 % 2, n % 16
                    W(pe, eC, n + 1, b)
                    for s, (lo, hi) in enumerate(SEG):
                        ins = pe.matmul(psB[:, 512 * par + lo:512 * par + hi], mix[:, s, k, eo, :], UT[:, n % 3, lo:hi], start=(n % 32 == 0 and s == 0), stop=False, skip_group_check=True)
                    ins.then_inc(pZ.s, 1)
                conv(0)
                for n in range(64):
                    if n < 63: conv(n + 1)
                    mixin(n)
                    if n % 32 == 31:
                        par = n // 32
                        for j in range(3):
                            for s, (lo, hi) in enumerate(SEG):
                                c0 = 2 + par - j + 2 * lo
                                ins = pe.matmul(psB[:, 512 * par + lo:512 * par + hi], mixu[:, s, j, :], nrmT[:, c0:c0 + 2 * (hi - lo) - 1:2], start=False, stop=(j == 2), skip_group_check=True)
                        ins.then_inc(pZ.s, 1)

        @block.scalar
        def _(act):
            act.wait_ge(s_set, 2)
            act.activation(sm8[:, 4:8], sm8[:, 0:4], ACT.Exp).then_inc(s_setp, 1)
            act.activation(sg[:, :], sg[:, :], ACT.Sqrt).then_inc(s_setp, 1)
            act.wait_ge(s_setp, 2)
            act.activation(sg[:, :], sg[:, :], ACT.Sqrt).then_inc(s_setp, 1)
            with act.Fori(0, NI) as b:
                def ln(L):
                    W(act, lnv, L + 1, b)
                    act.activation(std[:, :], var[:, :], ACT.Sqrt).then_inc(lns.s, 1)
                    W(act, pBT, L + 1, b)
                    act.activation(nrmT[:, 2:2 + T], psA[:, 0:T], ACT.Copy).then_inc(eBT.s, 1)
                ln(0)
                W(act, pWi, 1, b)
                act.activation(proj[:, :].rearrange("p (h w) -> p h w", h=2), psB[:, :].rearrange("p (h w) -> p h w", h=2)[:, :, 0:HALF], ACT.Copy).then_inc(eWi.s, 1)
                def exps(blk):
                    R = TOK_ROWS[blk]
                    W(act, mx, blk + 1, b)
                    act.activation(S[0:R, blk, :], S[0:R, blk, :], ACT.Exp, bias=small[0:R, blk:blk + 1], accum_out=small[0:R, 8 + blk:9 + blk]).then_inc(ex.s, 1)
                for blk in range(6):
                    Wd = T - 128 * blk
                    for r in range(STEPS):
                        st = STEPS * blk + r
                        W(act, sums, 4 * (st + 1), b)
                        act.activation(ring[:, st % NB, :, 0:Wd], ring[:, st % NB, :, 0:Wd], ACT.Tanh).then_inc(th.s, 1)
                        if blk and r == 8: exps(blk - 1)
                W(act, sums, 4 * 6 * STEPS + 1, b)
                act.activation(ring[:, 0, 0, 0:TAIL * TAIL], ring[:, 0, 0, 0:TAIL * TAIL], ACT.Tanh).then_inc(th.s, 1)
                exps(5)
                exps(6)
                ln(1)
                W(act, sub8, 1, b)
                act.activation(prob[:, :, :], logit[:, :, :], ACT.Exp).then_inc(exp8.s, 1)
                W(act, pGT, 1, b)
                act.activation(gateT[:, :], psA[0:8, 0:T], ACT.Copy).then_inc(eGT.s, 1)
                ln(2)
                for a in range(2):
                    W(act, zm, a + 1, b)
                    act.activation(zmin[:, :], zmin[:, :], ACT.Exp).then_inc(eq_exp.s, 1)
                ln(3)
                W(act, pU, 2, b)
                ps = psA[:, :].rearrange("p (a b c) -> p a b c", a=2, b=4)
                act.activation(U[:, :, 0:3, :], ps[:, :, 0:3, :], ACT.Copy).then_inc(eU.s, 1)
                act.activation(U[0:8, :, 3, :], ps[0:8, :, 3, :], ACT.Copy).then_inc(eU.s, 1)
                W(act, pR, 1, b)
                act.activation(res[:, :], psA[:, 0:T], ACT.Copy).then_inc(eR.s, 1)
                for n in range(0, 64, 2):
                    W(act, pC, n + 1, b)
                    if n >= 3: W(act, pZ, n - 2 + (n - 3) // 32, b)
                    act.activation(UT[:, n % 3, :], psS[:, n % 2, 0, 0:HALF], ACT.Copy).then_inc(eC.s, 1)
                    W(act, eC, n + 2, b)

        @block.vector
        def _(dve):
            class Chain:
                def __init__(self, b, base, K): self.n = 0; self.b = b; self.base = base; self.K = K
                def do(self, ins): self.n += 1; ins.then_inc(dch, 1)
                def sync(self): dve.wait_ge(dch, (self.K * self.b + self.base + self.n) if self.b is not None else self.n)
                def link(self, ins): self.do(ins); self.sync()
            c = Chain(None, 0, 0)
            dve.wait_ge(s_pc, 10)
            dve.wait_ge(s_ld, 16 * 14)
            dve.tensor_scalar(vhot[:, :, :], vhot[:, :, :], vcol[:, 0:1], None, ALU.mult).then_inc(s_set, 1)
            z, soft, hard, rem = lw[:, 8:12], sm8[:, 4:8], lw[:, 0:4], sm8[:, 8:9]
            c.link(dve.tensor_tensor(z, lw[:, 0:4], lw[:, 4:8], ALU.add))
            c.link(dve.tensor_reduce(sm8[:, 9:10], z, AX.X, ALU.max))
            dve.tensor_scalar(sm8[:, 0:4], z, sm8[:, 9:10], None, ALU.subtract).then_inc(s_set, 1)
            dve.wait_ge(s_setp, 3)
            c.link(dve.tensor_reduce(sm8[:, 10:11], soft, AX.X, ALU.add))
            c.link(dve.reciprocal(sm8[:, 10:11], sm8[:, 10:11]))
            c.link(dve.tensor_scalar(soft, soft, sm8[:, 10:11], None, ALU.mult))
            c.link(dve.tensor_reduce(sm8[:, 11:12], soft, AX.X, ALU.max))
            c.link(dve.tensor_scalar(hard, soft, sm8[:, 11:12], None, ALU.is_equal))
            c.link(dve.memset(rem, 1.0))
            for i in range(4):
                c.link(dve.tensor_tensor(hard[:, i:i + 1], hard[:, i:i + 1], rem, ALU.mult))
                c.link(dve.tensor_tensor(rem, rem, hard[:, i:i + 1], ALU.subtract))
            c.link(dve.tensor_tensor(hard, hard, soft, ALU.subtract))
            c.link(dve.tensor_tensor(hard, hard, soft, ALU.add))
            for i in range(4):
                c.do(dve.tensor_scalar(coef[:, i, :], sg[:, :], hard[:, i:i + 1], None, ALU.mult))
            c.sync()
            for i in range(4):
                dve.wait_ge(s_br, 48 * (i + 1))
                c.do(dve.tensor_tensor(msum, mp, mm_, ALU.add))
                c.do(dve.tensor_tensor(mdif, mp, mm_, ALU.subtract))
                c.sync()
                for k in range(NK):
                    for eo, m in enumerate((msum, mdif)):
                        if i == 0:
                            c.do(dve.tensor_scalar(mix[:, 0, k, eo, :], m[:, k, :], coef[:, 0, k:k + 1], None, ALU.mult))
                        else:
                            c.do(dve.scalar_tensor_tensor(out=mix[:, i, k, eo, :], in0=m[:, k, :], scalar=coef[:, i, k:k + 1], in1=mix[:, i - 1, k, eo, :], op0=ALU.mult, op1=ALU.add))
                if i == 0:
                    c.do(dve.tensor_scalar(mixu[:, 0, :, :], mu, hard[:, 0:1], None, ALU.mult))
                else:
                    c.do(dve.scalar_tensor_tensor(out=mixu[:, i, :, :].rearrange("p a b -> p (a b)"), in0=mu.rearrange("p a b -> p (a b)"), scalar=hard[:, i:i + 1], in1=mixu[:, i - 1, :, :].rearrange("p a b -> p (a b)"), op0=ALU.mult, op1=ALU.add))
                c.sync()
                dve.sem_inc(s_brf, 1) if False else c.link(dve.memset(rem, 1.0))
                dve.memset(rem, 1.0).then_inc(s_brf, 1)
            dve.wait_ge(s_brf, 4)
            c.link(dve.memset(vaug[:, :, 128:129], 1.0))
            base = c.n
            with dve.Fori(0, NI) as b:
                c = Chain(b, base, token_layers.K)
                def ln(L):
                    for t in tiles: c.do(dve.bn_stats(stats[:, t, :], tok[:, t, :]))
                    c.sync()
                    c.do(dve.memset(pad[:, 0:2], 0.0))
                    for t in tiles: c.do(dve.bn_aggr(mv[:, t, :], stats[:, t, :]))
                    c.sync()
                    dve.tensor_scalar(var[:, :], mv[:, :, 1], LN_EPS, None, ALU.add).then_inc(lnv.s, 1)
                    W(dve, lns, L + 1, b)
                    c.link(dve.reciprocal(std[:, :], std[:, :]))
                    for t in tiles:
                        ins = dve.tensor_scalar(nrm[:, t, :], tok[:, t, :], mv[:, t, 0:1], std[:, t:t + 1], ALU.subtract, ALU.mult)
                        if t < 6: c.do(ins)
                    c.sync()
                    ins.then_inc(lnB.s, 1)
                W(dve, pX, 1, b)
                dve.tensor_copy(tok[:, 0:6, :].rearrange("p a b -> p (a b)"), psA[:, 0:768]).then_inc(tT.s, 1)
                dve.tensor_copy(tok[0:TAIL, 6, :], psA[0:TAIL, 768:896]).then_inc(tT.s, 1)
                W(dve, tT, 2, b)
                ln(0)
                W(dve, eWi, 1, b)
                def evac(blk):
                    R = TOK_ROWS[blk]; Wd = T - 128 * blk; nch = 2 if Wd > 512 else 1; w = Wd // nch
                    W(dve, pS, blk + 1, b)
                    dve.tensor_copy(S[0:R, blk, 128 * blk:T].rearrange("p (h w) -> p h w", h=nch), psS[0:R, blk % 2, 0:nch, 0:w]).then_inc(Sev.s, 1)
                def filled(blk):
                    W(dve, pF, blk + 1, b)
                    if blk < 5:
                        c.link(dve.tensor_copy(S[:, blk + 1:6, 128 * blk:128 * blk + 128], psA[:, 0:128 * (5 - blk)].rearrange("p (t c) -> p t c", c=128)))
                    dve.tensor_copy(S[0:TAIL, 6, 128 * blk:128 * blk + 128], psA[0:TAIL, 128 * (5 - blk):128 * (6 - blk)]).then_inc(eF.s, 1)
                def rowmax(blk):
                    R = TOK_ROWS[blk]
                    W(dve, Sev, blk + 1, b)
                    W(dve, eF, min(blk + 1, 6), b)
                    dve.tensor_reduce(small[0:R, blk:blk + 1], S[0:R, blk, :], AX.X, ALU.max, negate=True).then_inc(mx.s, 1)
                def scale(blk):
                    R = TOK_ROWS[blk]
                    W(dve, ex, blk + 1, b)
                    c.link(dve.reciprocal(small[0:R, 16 + blk:17 + blk], small[0:R, 8 + blk:9 + blk]))
                    dve.tensor_scalar(S[0:R, blk, :], S[0:R, blk, :], small[0:R, 16 + blk:17 + blk], None, ALU.mult).then_inc(eP.s, 1)
                def ptev(blk):
                    R = TOK_ROWS[blk]
                    W(dve, pPT, blk + 1, b)
                    c.link(dve.tensor_copy(PT[:, 0:6, 0:R], psA[:, 0:768].rearrange("p (t c) -> p t c", c=128)[:, :, 0:R]))
                    dve.tensor_copy(PT[0:TAIL, 6, 0:R], psA[0:TAIL, 768:768 + R]).then_inc(ePT.s, 1)
                def addo(blk):
                    R = TOK_ROWS[blk]
                    W(dve, pO, blk + 1, b)
                    dve.tensor_tensor(tok[0:R, blk, :], tok[0:R, blk, :], psB[0:R, 0:128], ALU.add).then_inc(eO.s, 1)
                for blk in range(6):
                    Wd = T - 128 * blk
                    for r in range(STEPS):
                        st = STEPS * blk + r
                        dve.wait_ge(s_credit, (6 * STEPS + 1) * b + st + 1)
                        for q in range(4):
                            i = 128 * blk + 32 * q + r
                            dve.tensor_scalar(ring[:, st % NB, q, 0:Wd], proj[:, 128 * blk:T], proj[:, i:i + 1], None, ALU.add).then_inc(sums.s, 1)
                        if blk:
                            if r == 3: evac(blk - 1)
                            if r == 6: filled(blk - 1); rowmax(blk - 1)
                            if r == 12: scale(blk - 1)
                            if r == 17: ptev(blk - 1)
                            if r == 23: addo(blk - 1)
                dve.wait_ge(s_credit, (6 * STEPS + 1) * b + 6 * STEPS + 1)
                pj = proj[:, T - TAIL:T]
                dve.tensor_tensor(ring[:, 0, 0, 0:TAIL * TAIL].rearrange("p (a b) -> p a b", a=TAIL), pj.unsqueeze(1).to_broadcast([128, TAIL, TAIL]), pj.unsqueeze(2).to_broadcast([128, TAIL, TAIL]), ALU.add).then_inc(sums.s, 1)
                evac(5); filled(5); rowmax(5)
                evac(6); rowmax(6)
                scale(5); scale(6); ptev(5); addo(5); ptev(6); addo(6)
                W(dve, eO, 7, b)
                ln(1)
                W(dve, pL, 1, b)
                pl = psB[:, 512:568].rearrange("p (t e) -> p t e", e=8)
                rbb = rb[:, :].unsqueeze(1).to_broadcast([128, 6, 8])
                c.do(dve.tensor_tensor(logit[:, 0:6, :], pl[:, 0:6, :], rbb, ALU.add))
                c.do(dve.tensor_tensor(logit[0:TAIL, 6, :], pl[0:TAIL, 6, :], rb[0:TAIL, :], ALU.add))
                c.sync()
                c.link(dve.tensor_reduce(small[:, 24:31], logit[:, :, :], AX.X, ALU.max))
                bc = lambda a: a.unsqueeze(2).to_broadcast([128, NT, 8])
                dve.tensor_tensor(logit[:, :, :], logit[:, :, :], bc(small[:, 24:31]), ALU.subtract).then_inc(sub8.s, 1)
                W(dve, exp8, 1, b)
                c.link(dve.tensor_reduce(small[:, 32:39], prob[:, :, :], AX.X, ALU.add))
                c.link(dve.reciprocal(small[:, 32:39], small[:, 32:39]))
                c.link(dve.tensor_tensor(prob[:, :, :], prob[:, :, :], bc(small[:, 32:39]), ALU.mult))
                mine = prob[:, :, :].unsqueeze(3).to_broadcast([128, NT, 8, 8]); other = prob[:, :, :].unsqueeze(2).to_broadcast([128, NT, 8, 8])
                c.do(dve.tensor_tensor(gt[:, :, :, :], other, mine, ALU.is_gt))
                c.link(dve.tensor_tensor(eq[:, :, :, :], other, mine, ALU.is_equal))
                c.link(dve.tensor_tensor(eq[:, :, :, :], eq[:, :, :, :], lower[:, :, :].unsqueeze(1).to_broadcast([128, NT, 8, 8]), ALU.mult))
                c.link(dve.tensor_tensor(gt[:, :, :, :], gt[:, :, :, :], eq[:, :, :, :], ALU.add))
                c.link(dve.tensor_reduce(logit[:, :, :], gt[:, :, :, :], AX.X, ALU.add))
                c.link(dve.tensor_scalar(logit[:, :, :], logit[:, :, :], 2.0, None, ALU.is_lt))
                c.link(dve.tensor_tensor(prob[:, :, :], prob[:, :, :], logit[:, :, :], ALU.mult))
                c.link(dve.tensor_reduce(small[:, 40:47], prob[:, :, :], AX.X, ALU.add))
                c.link(dve.reciprocal(small[:, 40:47], small[:, 40:47]))
                dve.tensor_tensor(prob[:, :, :], prob[:, :, :], bc(small[:, 40:47]), ALU.mult).then_inc(gate.s, 1)
                W(dve, gate, 1, b)
                for t in tiles:
                    R = TOK_ROWS[t]
                    W(dve, pY, t + 1, b)
                    c.link(dve.tensor_tensor(tok[0:R, t, :], tok[0:R, t, :], psB[0:R, 512 * (t % 2):512 * (t % 2) + 128], ALU.add))
                    for e in range(8):
                        ins = dve.scalar_tensor_tensor(out=tok[0:R, t, :], in0=psS[0:R, t % 2, e // 4, 128 * (e % 4):128 * (e % 4) + 128], scalar=prob[0:R, t, e:e + 1], in1=tok[0:R, t, :], op0=ALU.mult, op1=ALU.add)
                        if e < 7: c.link(ins)
                    ins.then_inc(eY.s, 1)
                W(dve, eY, 7, b)
                ln(2)
                for a in range(2):
                    W(dve, pQ, a + 1, b)
                    ps = psS[:, a, :, 0:HALF]; v2 = lambda x: x.rearrange("p (h w) -> p h w", h=2)
                    c.link(dve.tensor_scalar(v2(zq), ps, bqk[:, a:a + 1], None, ALU.add))
                    dve.tensor_scalar(zmin[:, :], zq[:, :], 0.0, None, ALU.min).then_inc(zm.s, 1)
                    W(dve, eq_exp, a + 1, b)
                    dve.scalar_tensor_tensor(out=(qT, kT)[a][:, :], in0=zq[:, :], scalar=0.0, in1=zmin[:, :], op0=ALU.max, op1=ALU.add).then_inc(qk.s, 1)
                    W(dve, qk, a + 1, b)
                W(dve, pV, 1, b)
                c.do(dve.tensor_tensor(vaug[:, 0:6, 0:128], psA[:, 0:768].rearrange("p (t c) -> p t c", c=128), bv[:, :].unsqueeze(1).to_broadcast([128, 6, 128]), ALU.add))
                c.do(dve.memset(vaug[:, :, 128:129], 1.0))
                c.sync()
                dve.tensor_tensor(vaug[0:TAIL, 6, 0:128], psA[0:TAIL, 768:896], bv[0:TAIL, :], ALU.add).then_inc(eV.s, 1)
                for i in tiles:
                    R = TOK_ROWS[i]; Wd = T - 128 * i; nch = 2 if Wd > 512 else 1; w = Wd // nch
                    W(dve, pAT, i + 1, b)
                    ins = dve.tensor_copy(AT[0:R, ATo[i]:ATo[i] + Wd].rearrange("p (h w) -> p h w", h=nch), psS[0:R, i % 2, 0:nch, 0:w])
                    c.link(ins)
                    dve.tensor_tensor(AT[0:R, ATo[i]:ATo[i] + R], AT[0:R, ATo[i]:ATo[i] + R], causal[0:R, 0:R], ALU.mult).then_inc(eAT.s, 1)
                for t in tiles:
                    R = TOK_ROWS[t]; o = 512 * (t % 2)
                    W(dve, pN, t + 1, b)
                    c.link(dve.tensor_scalar(small[0:R, 48 + t:49 + t], psB[0:R, o + 128:o + 129], 1e-6, None, ALU.add))
                    c.link(dve.reciprocal(small[0:R, 48 + t:49 + t], small[0:R, 48 + t:49 + t]))
                    dve.scalar_tensor_tensor(out=tok[0:R, t, :], in0=psB[0:R, o:o + 128], scalar=small[0:R, 48 + t:49 + t], in1=tok[0:R, t, :], op0=ALU.mult, op1=ALU.add).then_inc(eN.s, 1)
                W(dve, eN, 7, b)
                ln(3)
                for n in range(64):
                    if n % 2:
                        W(dve, pC, n + 1, b)
                        W(dve, eC, n, b)
                        if n >= 3: W(dve, pZ, n - 2 + (n - 3) // 32, b)
                        dve.tensor_copy(UT[:, n % 3, :], psS[:, n % 2, 0, 0:HALF]).then_inc(eC.s, 1)
                    if n == 40 or n == 63:
                        par = int(n == 63)
                        W(dve, pZ, 33 * (par + 1), b)
                        if par == 0:
                            W(dve, eR, 1, b)
                        dve.tensor_tensor(res[:, par:T:2], res[:, par:T:2], psB[:, 512 * par:512 * par + HALF], ALU.add).then_inc(out_ready.s, 1)
                W(dve, out_ready, 2, b)
                dve.wait_ge(stored.s, 16 * b + 16)
                assert c.n == token_layers.K, c.n
token_layers.K = 203

def build(nc, ai, out, pairs):
    x1 = nc.dram_tensor("x1_scratch", (pairs, 2, 128, T), F32, kind="Internal").ap()
    conv_layers(nc, ai, x1, pairs)
    token_layers(nc, ai, x1.rearrange("p i c t -> (p i) c t"), out, 2 * pairs)

def kernel(**inputs):
    import numpy as _np
    import concourse.bacc as _bacc
    from concourse import mybir as _mybir
    from concourse.bass_utils import run_bass_kernel_spmd as _run

    v = {k: _np.asarray(a) for k, a in inputs.items()}
    taps = lambda w: w.reshape(128, 128, 9).transpose(1, 2, 0)
    phi = _np.zeros((2, 16, 128 + HALF), _np.float32)
    phi[:, :, 128:] = v["L3_ffn_phi"][:T].reshape(HALF, 2, 16).transpose(1, 2, 0)
    toep = phi.reshape(32, 128 + HALF)[:, 127 - _np.arange(128)[:, None] + _np.arange(HALF + 1)[None, :]].transpose(1, 0, 2)
    data = {
        "x": v["x"].reshape(8, 2, 128, T),
        "w0t": v["L0_conv_W"].reshape(4, 32, 128, 9).transpose(2, 3, 1, 0).reshape(128, 9, 128),
        "w0r": v["L0_conv_W"].reshape(128, -1),
        "w1t": taps(v["L1_conv_w1"]), "w2t": taps(v["L1_conv_w2"]),
        "gamma1": v["L1_conv_gamma1"], "gamma2": v["L1_conv_gamma2"], "beta1": v["L1_conv_beta1"], "beta2": v["L1_conv_beta2"],
        "mean1": v["L1_conv_mean1"], "mean2": v["L1_conv_mean2"], "var1": v["L1_conv_var1"], "var2": v["L1_conv_var2"],
        "wa": v["L2_attn_W"].T, "v": v["L2_attn_v"], "rw": v["L2_ffn_router_w"], "rb": v["L2_ffn_router_b"],
        "ew": v["L2_ffn_expert_w"].transpose(1, 0, 2).reshape(128, 1024), "eb": v["L2_ffn_expert_b"],
        "wqkv": v["L3_attn_W"].T, "bqkv": v["L3_attn_b"],
        "sigma": v["L3_ffn_sigma"], "lw": v["L3_ffn_log_weights"], "gum": v["L3_ffn_gumbel"], "toep": toep,
        "mp": v["L3_ffn_M_phi_plus"], "mm": v["L3_ffn_M_phi_minus"], "mu": v["L3_ffn_M_u"],
    }
    nc = _bacc.Bacc("TRN2", target_bir_lowering=False, num_devices=1)
    arrays, aps = {}, {}
    for name, a in data.items():
        a = _np.ascontiguousarray(a)
        arrays[f"in_{name}_dram"] = a
        aps[name] = nc.dram_tensor(f"in_{name}_dram", a.shape, _mybir.dt.from_np(a.dtype), kind="ExternalInput").ap()
    out = nc.dram_tensor("out_0_dram", (16, 128, T), _mybir.dt.float32, kind="ExternalOutput").ap()
    build(nc, aps, out, 8)
    r = _run(nc, [arrays], core_ids=[0])
    return r.results[0]["out_0_dram"].reshape(16, 128, 28, 28)
```

```python
from contextlib import ExitStack
import numpy as np
import concourse.bass as bass
from concourse import mybir
F32 = mybir.dt.float32
BF16 = mybir.dt.bfloat16
ALU = mybir.AluOpType
ACT = mybir.ActivationFunctionType
AX = mybir.AxisListType
RMAX = bass.bass_isa.ReduceOp.max

C = 128; HW = 28; T = HW * HW; PW = HW + 2; HALF = T // 2; ROWS = HW // 2
TAPS = 9; RING = 4; ROUND = 1.5 * 2.0 ** 23; LEVELS = 15.0
BN_EPS = 1e-5
KEPT_TAPS = [t for t in range(TAPS) if t not in (0, 8)]
VEC_SHARE = [3 if r % 2 == 0 else 2 for r in range(32)]
VEC_TILES = sum(VEC_SHARE); ACT_TILES = 4 * 32 - VEC_TILES

def conv_layers(nc, ai, x1, NP):
    with ExitStack() as ctx:
        sb = lambda n, s, d=F32: ctx.enter_context(nc.sbuf_tensor("c_" + n, s, d))
        pb = lambda n, s, d=F32: ctx.enter_context(nc.psum_tensor("c_" + n, s, d))
        sem = lambda n: ctx.enter_context(nc.semaphore("c_" + n))
        onehot = sb("onehot", [128, 63])
        group_avg = sb("group_avg", [128, 128])
        minus_half = sb("minus_half", [128, 128])
        zero_bf = sb("zero_bf", [128, 392 + 128], BF16)
        w0 = sb("w0", [128, TAPS, 128]); w0_neg = sb("w0_neg", [128, TAPS, 128]); w0_rows = sb("w0_rows", [128, TAPS * C])
        w0_sum = sb("w0_sum", [128, 1])
        wq1 = sb("wq1", [128, TAPS, 128]); wq2 = sb("wq2", [128, TAPS, 128]); wq2b = sb("wq2b", [128, TAPS, 128], BF16)
        wmax = sb("wmax", [128, 2]); wmax_all = sb("wmax_all", [128, 2]); wscale = sb("wscale", [128, 2])
        bn = sb("bn", [128, 8]); bn_std = sb("bn_std", [128, 2]); bn_scale = sb("bn_scale", [128, 2]); bn_shift = sb("bn_shift", [128, 2]); bn_q = sb("bn_q", [128, 2])
        xin = sb("xin", [128, 2, T])
        xn = sb("xn", [128, 2, PW, PW])
        rows3 = sb("rows3", [128, 2, PW, HW]); box = sb("box", [128, 2, HW, HW])
        ring = sb("ring", [128, RING, 4, 2 * T])
        stats = sb("stats", [128, 2, 2, 6]); mv = sb("mv", [128, 2, 2]); gmv = sb("gmv", [128, 2, 2]); pad = sb("pad", [128, 2])
        dev = sb("dev", [128, 2]); dev2 = sb("dev2", [128, 2]); gvar = sb("gvar", [128, 2]); gstd = sb("gstd", [128, 2]); grstd = sb("grstd", [128, 2])
        act1 = sb("act1", [128, 4, HALF]); actq = sb("actq", [128, 4, HALF]); xq = sb("xq", [128, 2, PW, PW], BF16)
        tmp = sb("tmp", [128, 4, HALF]); xout = sb("xout", [128, 2, T])
        acc = pb("acc", [128, 4, 512]); psg = pb("psg", [128, 512])

        s_ld = sem("weights_loaded"); s_const = sem("constants_ready"); s_vs = sem("vec_setup"); s_tanh = sem("tanh_ready"); s_mxa = sem("max_all_ready")
        s_x = sem("x_loaded"); s_stat = sem("stats_ready"); s_gmean = sem("group_mean_ready"); s_dev = sem("dev_ready")
        s_gdev = sem("group_dev_ready"); s_gvar = sem("group_var_ready"); s_gstd = sem("group_std_ready"); s_xn = sem("xn_ready")
        s_box = sem("box_ready"); s_pool = sem("pool_chain"); s_tv = sem("tiles_vec"); s_ta = sem("tiles_act"); s_free = sem("ring_free")
        s_acc = sem("distance_ready"); s_x1 = sem("x1_ready"); s_v = sem("vec_chain")
        s_c1 = sem("conv1_ready"); s_a1 = sem("act1_ready"); s_q = sem("quant_ready"); s_c2 = sem("conv2_ready"); s_o = sem("xout_ready"); s_st = sem("x1_stored")
        s_bstd = sem("bn_std_ready"); s_wact = sem("weights_act_neg")
        s_accr = sem("acc_read")
        block = ctx.enter_context(nc.Block())

        @block.sync
        def _(sp):
            sp.dma_start(w0[:, :, :], ai["w0t"]).then_inc(s_ld, 16)
            sp.dma_start(w0_rows[:, :], ai["w0r"]).then_inc(s_st, 16)
            sp.dma_start(wq1[:, :, :], ai["w1t"]).then_inc(s_ld, 16)
            sp.dma_start(wq2[:, :, :], ai["w2t"]).then_inc(s_ld, 16)
            for n, k in enumerate(["gamma1", "gamma2", "beta1", "beta2", "mean1", "mean2", "var1", "var2"]):
                sp.dma_start(bn[:, n:n + 1], ai[k].rearrange("(c o) -> c o", o=1)).then_inc(s_ld, 16)
            sp.dma_start(xin[:, :, :], ai["x"][0:1].rearrange("a i c t -> c (a i) t")).then_inc(s_x, 16)
            with sp.Fori(0, NP - 1) as p:
                sp.wait_ge(s_x1, p + 1)
                sp.dma_start(xin[:, :, :], ai["x"][bass.ds(p + 1, 1)].rearrange("a i c t -> c (a i) t")).then_inc(s_x, 16)
                sp.wait_ge(s_o, 4 * p + 4)
                sp.dma_start(x1[bass.ds(p, 1)].rearrange("a i c t -> c (a i) t"), xout[:, :, :]).then_inc(s_st, 16)
            sp.wait_ge(s_o, 4 * NP)
            sp.dma_start(x1[NP - 1:NP].rearrange("a i c t -> c (a i) t"), xout[:, :, :]).then_inc(s_st, 16)
            sp.wait_ge(s_st, 16 * NP + 16)

        @block.gpsimd
        def _(pool):
            pool.memset(onehot[:, :], 0.0).then_inc(s_pool, 1)
            pool.memset(group_avg[:, :], 0.25).then_inc(s_pool, 1)
            pool.memset(minus_half[:, :], -0.5).then_inc(s_pool, 1)
            pool.memset(zero_bf[:, :], 0.0).then_inc(s_pool, 1)
            pool.memset(pad[:, 1:2], 0.0).then_inc(s_accr, 4)
            pool.memset(xn[:, :, :, :], 0.0).then_inc(s_pool, 1)
            pool.memset(xq[:, :, :, :], 0.0).then_inc(s_pool, 1)
            pool.wait_ge(s_pool, 6)
            pool.affine_select(out=onehot[:, :], in_=onehot[:, :], compare_op=ALU.not_equal, fill=1.0, base=-31, pattern=[[1, 63]], channel_multiplier=0).then_inc(s_pool, 1)
            g3 = group_avg[:, :].rearrange("p (g k) -> p g k", k=4)
            pool.affine_select(out=g3, in_=g3, compare_op=ALU.is_ge, fill=0.0, base=0, pattern=[[-4, 32], [0, 4]], channel_multiplier=1).then_inc(s_pool, 1)
            pool.wait_ge(s_pool, 8)
            pool.affine_select(out=g3, in_=g3, compare_op=ALU.is_ge, fill=0.0, base=3, pattern=[[4, 32], [0, 4]], channel_multiplier=-1).then_inc(s_pool, 1)
            pool.wait_ge(s_pool, 9)
            pool.wait_ge(s_vs, 2)
            pool.partition_all_reduce(wmax_all[:, :], wmax[:, :], 128, RMAX).then_inc(s_mxa, 1)
            with pool.Fori(0, NP) as p:
                pool.wait_ge(s_xn, 2 * p + 2)
                k = 9
                K = 3
                def link(ins, n):
                    ins.then_inc(s_pool, 1)
                    pool.wait_ge(s_pool, K * p + 9 + n)
                link(pool.tensor_tensor(rows3[:, :, :, :], xn[:, :, :, 0:HW], xn[:, :, :, 1:1 + HW], ALU.add), 1)
                link(pool.tensor_tensor(rows3[:, :, :, :], rows3[:, :, :, :], xn[:, :, :, 2:2 + HW], ALU.add), 2)
                link(pool.tensor_tensor(box[:, :, :, :], rows3[:, :, 0:HW, :], rows3[:, :, 1:1 + HW, :], ALU.add), 3)
                pool.tensor_tensor(box[:, :, :, :], box[:, :, :, :], rows3[:, :, 2:2 + HW, :], ALU.add).then_inc(s_box, 1)

        @block.tensor
        def _(pe):
            pe.wait_ge(s_pool, 9)
            pe.matmul(psg[:, 0:4], group_avg[:, :], minus_half[:, 0:4], start=True, stop=True).then_inc(s_free, RING)
            with pe.Fori(0, NP) as p:
                pe.wait_ge(s_stat, 2 * p + 2)
                pe.matmul(psg[:, 0:4], group_avg[:, :], mv[:, :, :], start=True, stop=True).then_inc(s_gmean, 1)
                pe.wait_ge(s_dev, p + 1)
                pe.matmul(psg[:, 8:10], group_avg[:, :], dev2[:, :], start=True, stop=True).then_inc(s_gdev, 1)
                pe.wait_ge(s_accr, 4 * p + 4)
                for ch in range(4):
                    pe.matmul(acc[:, ch, 0:HALF], zero_bf[:, 0:128], zero_bf[:, 128:128 + HALF], start=True, stop=False, skip_group_check=True)
                with pe.Fori(0, 3) as dy:
                    with pe.Fori(0, 3) as dx:
                        j = 9 * p + 3 * dy + dx
                        vec = act = 0
                        for r in range(32):
                            vec += VEC_SHARE[r]; act += 4 - VEC_SHARE[r]
                            pe.wait_ge(s_tv, j * VEC_TILES + vec)
                            pe.wait_ge(s_ta, j * ACT_TILES + act)
                            for ch in range(4):
                                for g in range(4):
                                    mm = pe.matmul(acc[32 * g:32 * g + 32, ch, 0:HALF], onehot[:, 31 - r:63 - r], ring[:, r % RING, g, ch * HALF:(ch + 1) * HALF],
                                                   start=False, stop=False, skip_group_check=True)
                            mm.then_inc(s_free, 1)
                pe.wait_ge(s_box, p + 1)
                bx = box[:, :, :, :].rearrange("c i h w -> c (i h w)")
                for ch in range(4):
                    mm = pe.matmul(acc[:, ch, 0:HALF], minus_half[:, :], bx[:, ch * HALF:(ch + 1) * HALF], start=False, stop=True, skip_group_check=True)
                mm.then_inc(s_acc, 1)
                pe.wait_ge(s_x1, p + 1)
                for im in range(2):
                    for h in range(2):
                        for t in KEPT_TAPS:
                            y, x = t // 3, t % 3
                            mm = pe.matmul(acc[:, 2 * im + h, 0:HALF], wq1[:, t, :], xn[:, im, y + ROWS * h:y + ROWS * (h + 1), x:x + HW],
                                           start=(t == KEPT_TAPS[0]), stop=(t == KEPT_TAPS[-1]))
                        mm.then_inc(s_c1, 1)
                for im in range(2):
                    pe.wait_ge(s_q, 4 * p + 2 * im + 2)
                    for h in range(2):
                        for t in KEPT_TAPS:
                            y, x = t // 3, t % 3
                            mm = pe.matmul(acc[:, 2 * im + h, 0:HALF], wq2b[:, t, :], xq[:, im, y + ROWS * h:y + ROWS * (h + 1), x:x + HW],
                                           start=(t == KEPT_TAPS[0]), stop=(t == KEPT_TAPS[-1]))
                        mm.then_inc(s_c2, 1)

        @block.scalar
        def _(act):
            act.wait_ge(s_ld, 16 * 11)
            act.activation(wq1[:, :, :], wq1[:, :, :], ACT.Tanh).then_inc(s_tanh, 1)
            act.activation(wq2[:, :, :], wq2[:, :, :], ACT.Tanh).then_inc(s_tanh, 1)
            act.activation(w0_neg[:, :, :], w0[:, :, :], ACT.Copy, scale=-1.0).then_inc(s_wact, 1)
            act.wait_ge(s_vs, 3)
            act.activation(bn_std[:, :], bn[:, 6:8], ACT.Sqrt).then_inc(s_bstd, 1)
            act.wait_ge(s_wact, 1)
            with act.Fori(0, NP) as p:
                act.wait_ge(s_gvar, p + 1)
                act.activation(gstd[:, :], gvar[:, :], ACT.Sqrt).then_inc(s_gstd, 1)
                act.wait_ge(s_xn, 2 * p + 2)
                with act.Fori(0, 3) as dy:
                    with act.Fori(0, 3) as dx:
                        j = 9 * p + 3 * dy + dx
                        for r in range(32):
                            act.wait_ge(s_free, j * 32 + r + 1)
                            for g in range(VEC_SHARE[r], 4):
                                act.activation(ring[:, r % RING, g, :].rearrange("c (i h w) -> c i h w", i=2, h=HW), xn[:, :, bass.ds(dy, HW), bass.ds(dx, HW)], ACT.Relu,
                                               bias=w0_neg[:, bass.ds(3 * dy + dx, 1), 4 * r + g]).then_inc(s_ta, 1)
                for c in range(4):
                    act.wait_ge(s_c1, 4 * p + c + 1)
                    act.activation(act1[:, c, :], acc[:, c, 0:HALF], ACT.Relu, scale=bn_q[:, 0:1], bias=bn_shift[:, 0:1]).then_inc(s_a1, 1)

        @block.vector
        def _(dve):
            n = [0]
            def link(ins):
                n[0] += 1
                ins.then_inc(s_v, 1)
                dve.wait_ge(s_v, n[0])
            dve.wait_ge(s_tanh, 2)
            dve.wait_ge(s_st, 16)
            for q, wq in enumerate((wq1, wq2)):
                dve.tensor_reduce(wmax[:, q:q + 1], wq[:, :, :], AX.XY, ALU.max, apply_absolute_value=True).then_inc(s_vs, 1)
            link(dve.tensor_scalar(bn[:, 6:8], bn[:, 6:8], BN_EPS, None, ALU.add))
            dve.tensor_reduce(w0_sum[:, :], w0_rows[:, :], AX.X, ALU.add).then_inc(s_vs, 1)
            dve.wait_ge(s_vs, 3)
            dve.wait_ge(s_mxa, 1)
            link(dve.tensor_scalar(wmax_all[:, :], wmax_all[:, :], 2.0, None, ALU.mult))
            link(dve.reciprocal(wscale[:, :], wmax_all[:, :]))
            for q, wq in enumerate((wq1, wq2)):
                link(dve.tensor_scalar(wq[:, :, :], wq[:, :, :], wscale[:, q:q + 1], 0.5, ALU.mult, ALU.add))
                link(dve.tensor_scalar(wq[:, :, :], wq[:, :, :], LEVELS, ROUND, ALU.mult, ALU.add))
                link(dve.tensor_scalar(wq[:, :, :], wq[:, :, :], ROUND, 2.0, ALU.subtract, ALU.mult))
                link(dve.tensor_scalar((wq1, wq2b)[q][:, :, :], wq[:, :, :], LEVELS, None, ALU.subtract))
            dve.wait_ge(s_bstd, 1)
            link(dve.reciprocal(bn_std[:, :], bn_std[:, :]))
            link(dve.tensor_tensor(bn_scale[:, :], bn[:, 0:2], bn_std[:, :], ALU.mult))
            link(dve.tensor_tensor(bn_shift[:, :], bn[:, 4:6], bn_scale[:, :], ALU.mult))
            link(dve.tensor_tensor(bn_shift[:, :], bn[:, 2:4], bn_shift[:, :], ALU.subtract))
            link(dve.tensor_scalar(bn_q[:, 0:1], bn_scale[:, 0:1], 1.0 / LEVELS, None, ALU.mult))
            link(dve.tensor_scalar(bn_q[:, 1:2], bn_scale[:, 1:2], 1.0 / LEVELS ** 2, None, ALU.mult))
            dve.wait_ge(s_pool, 9)
            dve.wait_ge(s_accr, 4)
            base = n[0]
            K = 28
            with dve.Fori(0, NP) as p:
                n = [0]
                def link(ins):
                    n[0] += 1
                    ins.then_inc(s_v, 1)
                    dve.wait_ge(s_v, K * p + base + n[0])
                dve.wait_ge(s_x, 16 * p + 16)
                for im in range(2):
                    for h in range(2):
                        link(dve.bn_stats(stats[:, im, h, :], xin[:, im, h * HALF:(h + 1) * HALF]))
                n[0] += 1; dve.memset(pad[:, 0:1], 0.0).then_inc(s_v, 1)
                for im in range(2):
                    dve.bn_aggr(mv[:, im, :], stats[:, im, :, :]).then_inc(s_stat, 1)
                dve.wait_ge(s_gmean, p + 1)
                link(dve.tensor_copy(gmv[:, :, :], psg[:, 0:4].rearrange("c (i k) -> c i k", i=2)))
                dve.wait_ge(s_stat, 2 * p + 2)
                link(dve.tensor_tensor(dev[:, :], mv[:, :, 0], gmv[:, :, 0], ALU.subtract))
                dve.tensor_tensor(dev2[:, :], dev[:, :], dev[:, :], ALU.mult).then_inc(s_dev, 1)
                dve.wait_ge(s_gdev, p + 1)
                link(dve.tensor_tensor(gvar[:, :], gmv[:, :, 1], psg[:, 8:10], ALU.add))
                dve.tensor_scalar(gvar[:, :], gvar[:, :], 1e-5, None, ALU.add).then_inc(s_gvar, 1)
                dve.wait_ge(s_gstd, p + 1)
                link(dve.reciprocal(grstd[:, :], gstd[:, :]))
                for im in range(2):
                    dve.tensor_scalar(xn[:, im, 1:1 + HW, 1:1 + HW], xin[:, im, :].rearrange("c (h w) -> c h w", h=HW), gmv[:, im, 0:1], grstd[:, im:im + 1], ALU.subtract, ALU.mult).then_inc(s_xn, 1)
                dve.wait_ge(s_xn, 2 * p + 2)
                n[0] += 1; dve.memset(pad[:, 0:1], 0.0).then_inc(s_v, 1)
                with dve.Fori(0, 3) as dy:
                    with dve.Fori(0, 3) as dx:
                        j = 9 * p + 3 * dy + dx
                        for r in range(32):
                            dve.wait_ge(s_free, j * 32 + r + 1)
                            for g in range(VEC_SHARE[r]):
                                dve.tensor_scalar(ring[:, r % RING, g, :].rearrange("c (i h w) -> c i h w", i=2, h=HW), xn[:, :, bass.ds(dy, HW), bass.ds(dx, HW)],
                                                  w0[:, bass.ds(3 * dy + dx, 1), 4 * r + g], 0.0, ALU.subtract, ALU.max).then_inc(s_tv, 1)
                dve.wait_ge(s_acc, p + 1)
                dve.wait_ge(s_box, p + 1)
                link(dve.tensor_scalar(tmp[:, :, :], acc[:, :, 0:HALF], -2.0, w0_sum[:, 0:1], ALU.mult, ALU.subtract))
                for im in range(2):
                    ins = dve.tensor_tensor(xn[:, im, 1:1 + HW, 1:1 + HW], xin[:, im, :].rearrange("c (h w) -> c h w", h=HW),
                                      tmp[:, 2 * im:2 * im + 2, :].rearrange("c a (h w) -> c (a h) w", w=HW), ALU.add)
                    if im == 0: link(ins)
                ins.then_inc(s_x1, 1)
                dve.wait_ge(s_x1, p + 1)
                for c in range(4):
                    im, h = c // 2, c % 2
                    dve.wait_ge(s_a1, 4 * p + c + 1)
                    link(dve.tensor_scalar(actq[:, c, :], act1[:, c, :], 1.0, LEVELS, ALU.min, ALU.mult))
                    dve.tensor_scalar(xq[:, im, 1 + ROWS * h:1 + ROWS * (h + 1), 1:1 + HW], actq[:, c, :].rearrange("c (h w) -> c h w", w=HW), ROUND, ROUND, ALU.add, ALU.subtract).then_inc(s_q, 1)
                for c in range(4):
                    im, h = c // 2, c % 2
                    dve.wait_ge(s_c2, 4 * p + c + 1)
                    ins = dve.scalar_tensor_tensor(out=tmp[:, c, :].rearrange("c (h w) -> c h w", w=HW), in0=acc[:, c, 0:HALF].rearrange("c (h w) -> c h w", w=HW), scalar=bn_q[:, 1:2],
                                                   in1=xn[:, im, 1 + ROWS * h:1 + ROWS * (h + 1), 1:1 + HW], op0=ALU.mult, op1=ALU.add)
                    ins.then_inc(s_accr, 1)
                    dve.wait_ge(s_accr, 4 * p + c + 5)
                    link(dve.tensor_scalar(tmp[:, c, :], tmp[:, c, :], bn_shift[:, 1:2], 0.0, ALU.add, ALU.max))
                    link(dve.tensor_scalar(tmp[:, c, :], tmp[:, c, :], 1.0, LEVELS, ALU.min, ALU.mult))
                    link(dve.tensor_scalar(tmp[:, c, :], tmp[:, c, :], ROUND, ROUND, ALU.add, ALU.subtract))
                    if c == 0:
                        dve.wait_ge(s_st, 16 * p + 16)
                    dve.tensor_scalar(xout[:, im, h * HALF:(h + 1) * HALF], tmp[:, c, :], 1.0 / LEVELS, None, ALU.mult).then_inc(s_o, 1)
                assert n[0] == K, n[0]

NT = 7
TOK_ROWS = [128] * 6 + [16]
TAIL = TOK_ROWS[-1]
STEPS = 32
RINGS = 3
EXPERTS = 8
NK = 16
SEG = [(196, 392), (98, 196), (49, 98), (0, 49)]
HALVES = [((196, 392), [0]), ((0, 196), [1, 2, 3])]
QUART = HALF // 2
ORDER = [0, 4, 1, 3, 2, 5, 6]
POS = {blk: pos for pos, blk in enumerate(ORDER)}
CORNER_AT = 480
ST = [128, 128, 128, 8]
MIXES = 4
LN_EPS = 1e-5


def width(blk):
    wd = T - 128 * blk
    n = 2 if wd > 512 else 1
    return wd, n, wd // n


def buffer_of(blk):
    return 0 if width(blk)[1] == 2 else 1


LEAD_DVE = 3
LEAD_ACT = 1
AT_TAIL = dict(evac=-1, fill=1, rowmax=2, exp=3, scale=4, pt5=5, ptev5=6, out5=7, add5=8, out6=9, add6=10)
AT_EVAC = 1
AT_BLOCK = [32, 96, 160, 167, 174]
AT_SOFT = dict(fill=2, rowmax=3, exp=4, scale=5, pt=6, ptev=7, out=8, add=9)
LN_AT = dict(stats=0, aggr=1, norm=3, turn=4, evac=5)
AT_LN = [11, 44, 80]
AT_MOE = dict(logits=17, bias_add=18, exp=19, rank=20, rank2=21, gate=22, turn=23, evac=24, bias=25, bias_used=26, y=27)
AT_LIN = dict(q=50, zq=51, eq=52, qout=53, k=52, zk=53, ek=54, kout=55, v=54, vout=55, a=56, n=71)
AT_STU = dict(u=86, uev=87, res=88, resev=89, conv=91)
AT_NEXT = dict(x=108, tok=109, ln=110, wi=116, wiev=117)


def token_layers(nc, ai, x1, out_dram, NI):
    mixd = nc.dram_tensor("mix_scratch", (2 * NK, 128, 4, 128), F32, kind="Internal").ap()
    with ExitStack() as ctx:
        sb = lambda n, s, d=F32: ctx.enter_context(nc.sbuf_tensor("t_" + n, s, d))
        pb = lambda n, s, d=F32: ctx.enter_context(nc.psum_tensor("t_" + n, s, d))
        sem = lambda n: ctx.enter_context(nc.semaphore("t_" + n))
        toep = sb("toep", [128, 2 * NK, HALF + 1])
        mixr = sb("mixr", [128, MIXES, 4, 128])
        mixu = sb("mixu", [128, 4, 3, 128])
        ident = sb("ident", [128, 128]); causal = sb("causal", [128, 128]); vhot = sb("vhot", [128, 63]); vcol = sb("vcol", [128, 1])
        wa = sb("wa", [128, 128]); rw = sb("rw", [128, 8]); rb = sb("rb", [128, 8]); eb = sb("eb", [8, 128]); lower = sb("lower", [128, 8, 8])
        wqkv = sb("wqkv", [128, 384]); bqk = sb("bqk", [128, 2]); bv = sb("bv", [128, 128])
        ew = sb("ew", [128, 1024]); half7 = sb("half7", [128, NT])
        sg = sb("sg", [128, 16]); lw = sb("lw", [128, 12]); sm8 = sb("sm8", [128, 12]); coef = sb("coef", [128, 4, 16])
        tok2 = sb("tok", [128, 2, NT, 128]); nrm2 = sb("nrm", [128, 2, NT, 128]); proj2 = sb("proj", [128, 2, T]); nrmT = sb("nrmT", [128, T + 2])
        stats = sb("stats", [128, NT, 6]); mv = sb("mv", [128, NT, 2]); var = sb("var", [128, NT]); rstd = sb("rstd", [128, NT])
        small = sb("small", [128, 64]); pad = sb("pad", [128, 8]); corner = sb("corner", [128, TAIL * TAIL])
        SW, RW = NT * T, RINGS * 4 * T
        arena = sb("arena", [128, SW + RW + NT * 128])
        DW = 2 * 784 + NT * 129 + sum(T - 128 * i for i in range(NT))
        side = sb("side", [128, DW])
        U = sb("U", [128, 2, 4, 128]); UT = sb("UT", [128, 3, HALF]); res = sb("res", [128, T])
        def carver(t, size):
            off = [0]
            def carve(shape, parts=128):
                n = int(np.prod(shape)); a = t[0:parts, off[0]:off[0] + n]; off[0] += n
                assert off[0] <= size
                if len(shape) == 1: return a
                names = "abcd"[:len(shape)]
                return a.rearrange(f"p ({' '.join(names)}) -> p {' '.join(names)}", **{c: s for c, s in zip(names, shape)})
            return carve
        carve = carver(arena, SW + RW + NT * 128)
        mp = carve([NK, 128]); mm_ = carve([NK, 128]); msum = carve([NK, 128]); mdif = carve([NK, 128]); mrun = carve([NK, 2, 128]); mu = carve([3, 128])
        carve = carver(arena, SW + RW + NT * 128)
        S = carve([NT, T]); ring = carve([RINGS, 4, T]); PT = carve([NT, 128])
        carve = carver(side, DW)
        logit = carve([NT, 8]); prob = carve([NT, 8]); gt = carve([NT, 8, 8]); eq = carve([NT, 8, 8]); gateT = carve([T], 8)
        carve = carver(side, DW)
        qT = carve([T]); kT = carve([T]); vaug = carve([NT, 129]); ATw = sum(T - 128 * i for i in range(NT)); AT = carve([ATw])
        zq, zmin = AT[:, 0:T], AT[:, T:2 * T]
        ATo = [sum(T - 128 * k for k in range(i)) for i in range(NT)]

        psS = pb("psS", [128, 2, 2, 512]); psA = pb("psA", [128, 1024]); psB = pb("psB", [128, 1024])

        class Ev:
            def __init__(self, name, k, base=0): self.s = sem(name); self.k = k; self.base = base
        s_ld = sem("weights_loaded"); s_br = sem("branch_loaded"); s_brf = sem("branch_used"); s_mst = sem("mix_stored"); s_pc = sem("pool_chain"); s_set = sem("vec_setup"); s_setp = sem("act_setup")
        s_credit = sem("ring_free"); s_mrun = sem("mix_summed")
        dch = sem("vec_chain")
        x_in = Ev("x_in", 16); pX = Ev("x_turned", 1); tT = Ev("tokens_ready", 2)
        lnv = Ev("ln_var", 3); lns = Ev("ln_rstd", 3); lnB = Ev("ln_out", 3); pBT = Ev("ln_turned", 3); eBT = Ev("ln_channels", 3)
        lnv0 = Ev("ln0_var", 1); lns0 = Ev("ln0_rstd", 1); lnB0 = Ev("ln0_out", 1); pBT0 = Ev("ln0_turned", 1); eBT0 = Ev("ln0_channels", 1)
        pWi = Ev("proj_made", 1); eWi = Ev("proj_ready", 1)
        sums = Ev("sums", 6 * STEPS * 4 + 1); th = Ev("tanhs", 6 * STEPS + 1)
        pS = Ev("scores", 7); Sev = Ev("scores_out", 7); pF = Ev("fills", 6); eF = Ev("fills_out", 6); mx = Ev("row_max", 7); ex = Ev("exps", 7); eP = Ev("probs", 7); pPT = Ev("probs_turned", 7); ePT = Ev("probs_turned_out", 7)
        pO = Ev("attended", 7); eO = Ev("attention_added", 7)
        pL = Ev("logits", 1); sub8 = Ev("logits_less_max", 1); exp8 = Ev("logits_exp", 1); gate = Ev("gates", 1); pGT = Ev("gates_turned", 1); eGT = Ev("gates_turned_out", 1)
        pEB = Ev("expert_bias", 1); eEB = Ev("expert_bias_added", 1); pY = Ev("expert_out", 14); eY = Ev("expert_added", 14)
        pQ = Ev("qk_made", 2); zm = Ev("qk_min", 2); zexp = Ev("qk_exp", 2); qk = Ev("qk", 2); pV = Ev("v_made", 1); eV = Ev("v", 1)
        pAT = Ev("pairs", 7); eAT = Ev("pairs_out", 7); pN = Ev("lin_out", 7); eN = Ev("lin_added", 7)
        pU = Ev("times_turned", 2); eU = Ev("times", 2); pR = Ev("rest_turned", 1); eR = Ev("rest", 1); pC = Ev("filtered", 64); eC = Ev("filtered_out", 64); pZ = Ev("mixed", 64, MIXES); pAR = Ev("spectral", 2)
        out_ready = Ev("out_ready", 2); stored = Ev("stored", 16, 16)
        mix_in = [Ev(f"mix_in{i}", 16 * 4 * NK // MIXES) for i in range(MIXES)]
        block = ctx.enter_context(nc.Block())

        def W(e, ev, k, b):
            v = ev.k * b + (ev.base + k)
            if not isinstance(v, int) or v > 0:
                e.wait_ge(ev.s, v)

        def in_step(slot, due, tracks):
            for n, track in enumerate(tracks):
                while due[n] is not None and due[n] <= slot:
                    due[n] = next(track, None)

        def passes(e, prologue, one_pass, last):
            prologue()
            one_pass(0, 0, True, False)
            trips = (NI - 2) // 2
            with e.Fori(0, trips) as bb:
                one_pass(2 * bb + 1, 1, False, False, bb)
                one_pass(2 * bb + 2, 0, False, False, bb)
            one_pass(NI - 1, 1, False, True)
            last()

        tiles = range(NT)

        @block.sync
        def _(sp):
            for dst, src in ((wa[:, :], ai["wa"]), (rw[:, :], ai["rw"]), (eb[:, :], ai["eb"]), (wqkv[:, :], ai["wqkv"]), (ew[:, :], ai["ew"]),
                             (rb[:, :], ai["rb"].partition_broadcast(128)), (bv[:, :], ai["bqkv"][256:384].partition_broadcast(128)),
                             (bqk[:, 0:1], ai["bqkv"][0:128].rearrange("(c o) -> c o", o=1)), (bqk[:, 1:2], ai["bqkv"][128:256].rearrange("(c o) -> c o", o=1)),
                             (vcol[:, :], ai["v"].rearrange("(c o) -> c o", o=1)),
                             (sg[:, :], ai["sigma"].partition_broadcast(128)), (lw[:, 0:4], ai["lw"].partition_broadcast(128)), (lw[:, 4:8], ai["gum"].partition_broadcast(128))):
                sp.dma_start(dst, src).then_inc(s_ld, 16)
            for i in range(4):
                if i:
                    sp.wait_ge(s_brf, i)
                sp.dma_start(mp, ai["mp"][i].rearrange("k d e -> d k e")).then_inc(s_br, 16)
                sp.dma_start(mm_, ai["mm"][i].rearrange("k d e -> d k e")).then_inc(s_br, 16)
                sp.dma_start(mu, ai["mu"][i].rearrange("k d e -> d k e")).then_inc(s_br, 16)
                if i == 0:
                    sp.dma_start(toep[:, :, :], ai["toep"]).then_inc(s_ld, 16)
                sp.wait_ge(s_mrun, i + 1)
                sp.dma_start(mixd[:, :, i, :].rearrange("n d e -> d n e"), mrun.rearrange("p a b c -> p (a b) c")).then_inc(s_mst, 16)
            sp.wait_ge(s_mst, 64)

            def load_x(b, p):
                W(sp, sums, 1, b - 1)
                sp.dma_start(proj2[:, p, :], x1[bass.ds(b, 1)].rearrange("a c t -> c (a t)")).then_inc(x_in.s, 16)
            def rest(d):
                for u in range(4 * NK):
                    half, n = divmod(u, 2 * NK)
                    m0, m1 = HALVES[half][1][0], HALVES[half][1][-1] + 1
                    W(sp, pZ, u - MIXES + 1, d)
                    sp.dma_start(mixr[:, u % MIXES, m0:m1, :], mixd[n, :, m0:m1, :]).then_inc(mix_in[u % MIXES].s, 16)
                W(sp, out_ready, 2, d)
                sp.dma_start(out_dram[bass.ds(d, 1)].rearrange("a c t -> c (a t)"), res[:, :]).then_inc(stored.s, 16)
            def one_pass(b, p, first, last, bb=None):
                if not last: load_x(b + 1, 1 - p)
                if not first: rest(b - 1)
            passes(sp, lambda: load_x(0, 0), one_pass, lambda: rest(NI - 1))
            W(sp, stored, 0, NI)

        @block.gpsimd
        def _(pool):
            pool.memset(ident[:, :], 0.0).then_inc(s_pc, 1)
            pool.memset(causal[:, :], 1.0).then_inc(s_pc, 1)
            pool.memset(vhot[:, :], 0.0).then_inc(s_pc, 1)
            pool.memset(lower[:, :, :], 1.0).then_inc(s_pc, 1)
            pool.memset(tok2[:, :, :, :], 0.0).then_inc(s_pc, 1)
            pool.memset(nrmT[:, :], 0.0).then_inc(s_pc, 1)
            pool.memset(half7[:, :], -0.5).then_inc(s_pc, 1)
            pool.wait_ge(s_pc, 7)
            pool.affine_select(out=ident[:, :], in_=ident[:, :], compare_op=ALU.not_equal, fill=1.0, base=0, pattern=[[-1, 128]], channel_multiplier=1).then_inc(s_pc, 1)
            pool.affine_select(out=causal[:, :], in_=causal[:, :], compare_op=ALU.is_ge, fill=0.0, base=0, pattern=[[1, 128]], channel_multiplier=-1).then_inc(s_pc, 1)
            pool.affine_select(out=vhot[:, :], in_=vhot[:, :], compare_op=ALU.not_equal, fill=1.0, base=-31, pattern=[[1, 63]], channel_multiplier=0).then_inc(s_pc, 1)
            pool.affine_select(out=lower[:, :, :], in_=lower[:, :, :], compare_op=ALU.is_gt, fill=0.0, base=0, pattern=[[1, 8], [-1, 8]], channel_multiplier=0).then_inc(s_pc, 1)

            def root(ready, done, k, b):
                W(pool, ready, k, b)
                pool.tensor_tensor(rstd[:, :], var[:, :], half7[:, :], ALU.pow).then_inc(done.s, 1)
            pool.wait_ge(s_pc, 11)
            def one_pass(b, p, first, last, bb=None):
                if not first:
                    for k in range(3): root(lnv, lns, k + 1, b - 1)
                if not last: root(lnv0, lns0, 1, b + 1)
            def rest():
                for k in range(3): root(lnv, lns, k + 1, NI - 1)
            passes(pool, lambda: root(lnv0, lns0, 1, 0), one_pass, rest)

        @block.tensor
        def _(pe):
            pe.wait_ge(s_pc, 11)
            pe.wait_ge(s_set, 1)
            pe.matmul(psB[0:32, 0:8], ident[:, 0:32], ident[:, 0:8], start=True, stop=True).then_inc(s_credit, RINGS)
            pe.matmul(psB[0:32, 0:8], ident[:, 0:32], ident[:, 0:8], start=True, stop=True).then_inc(pZ.s, pZ.base)
            pe.matmul(psB[0:32, 0:8], ident[:, 0:32], ident[:, 0:8], start=True, stop=True).then_inc(stored.s, stored.base)

            def transposes(src_of, dst_of, ev, ns=tiles):
                for t in ns:
                    ins = pe.transpose(dst_of(t), src_of(t), ident[0:src_of(t).shape[0], 0:src_of(t).shape[0]])
                ins.then_inc(ev.s, 1)

            def next_image(b, p):
                tok, nrm, proj = tok2[:, p], nrm2[:, p], proj2[:, p]
                yield AT_NEXT["x"]
                W(pe, x_in, 16, b)
                W(pe, eO, 2, b - 1)
                transposes(lambda t: proj[:, 128 * t:128 * t + TOK_ROWS[t]], lambda t: psA[0:TOK_ROWS[t], 128 * t:128 * t + 128], pX)
                yield AT_NEXT["ln"] + LN_AT["turn"]
                W(pe, tT, 2, b)
                W(pe, lnB0, 1, b)
                transposes(lambda t: nrm[0:TOK_ROWS[t], t, :], lambda t: psA[:, 128 * t:128 * t + TOK_ROWS[t]], pBT0)
                yield AT_NEXT["wi"]
                W(pe, eBT0, 1, b)
                for h in range(2):
                    ins = pe.matmul(psA[:, 512 * h:512 * h + HALF], wa[:, :], proj[:, HALF * h:HALF * (h + 1)], start=True, stop=True)
                ins.then_inc(pWi.s, 1)

            def fill(blk, b, last=True):
                W(pe, Sev, POS[blk] + 1, b)
                if blk: W(pe, ePT, blk, b)
                if blk == 2 and not last: W(pe, eWi, 1, b + 1)
                transposes(lambda t: S[:, blk, 128 * t:128 * t + TOK_ROWS[t]], lambda t: psA[0:TOK_ROWS[t], 128 * (t - blk - 1):128 * (t - blk)], pF, range(blk + 1, NT))
            def turn_probs(blk, b):
                R = TOK_ROWS[blk]; pitch = R
                if blk < 6:
                    W(pe, eF, min(blk + 1, 6), b)
                    W(pe, eP, blk + 1 if blk < 5 else 7, b)
                transposes(lambda t: S[0:R, blk, 128 * t:128 * t + TOK_ROWS[t]], lambda t: psA[0:TOK_ROWS[t], pitch * t:pitch * t + R], pPT)
            def attend(blk, b, nrm):
                R = TOK_ROWS[blk]
                W(pe, ePT, blk + 1, b)
                if blk: W(pe, eO, blk, b)
                for t in tiles:
                    ins = pe.matmul(psA[0:R, 896:1024], PT[0:TOK_ROWS[t], t, 0:R], nrm[0:TOK_ROWS[t], t, :], start=(t == 0), stop=(t == 6))
                ins.then_inc(pO.s, 1)
            def soft(blk, b, p, last):
                s0 = AT_BLOCK[blk]
                yield s0 + AT_SOFT["fill"]
                fill(blk, b, last)
                yield s0 + AT_SOFT["pt"]
                turn_probs(blk, b)
                yield s0 + AT_SOFT["out"]
                attend(blk, b, nrm2[:, p])
            def tail(d, q):
                yield AT_TAIL["fill"]
                fill(5, d)
                yield AT_TAIL["pt5"]
                turn_probs(5, d)
                yield AT_TAIL["out5"]
                attend(5, d, nrm2[:, q])
                turn_probs(6, d)
                yield AT_TAIL["out6"]
                attend(6, d, nrm2[:, q])

            def rest(d, q):
                tok, nrm = tok2[:, q], nrm2[:, q]
                def ln(L):
                    W(pe, lnB, L + 1, d)
                    transposes(lambda t: nrm[0:TOK_ROWS[t], t, :], lambda t: psB[:, 128 * t:128 * t + TOK_ROWS[t]], pBT)
                yield AT_LN[0] + LN_AT["turn"]
                ln(0)
                yield AT_MOE["logits"]
                W(pe, eBT, 1, d)
                for t in tiles:
                    ins = pe.matmul(psB[0:TOK_ROWS[t], 8 * t:8 + 8 * t], nrmT[:, 2 + 128 * t:2 + 128 * t + TOK_ROWS[t]], rw[:, :], start=True, stop=True)
                ins.then_inc(pL.s, 1)
                yield AT_MOE["turn"]
                W(pe, gate, 1, d)
                transposes(lambda t: prob[0:TOK_ROWS[t], t, :], lambda t: psB[0:8, 128 * t:128 * t + TOK_ROWS[t]], pGT)
                yield AT_MOE["bias"]
                W(pe, eGT, 1, d)
                for t in tiles:
                    ins = pe.matmul(psB[0:TOK_ROWS[t], 128 * t:128 * t + 128], gateT[:, 128 * t:128 * t + TOK_ROWS[t]], eb[:, :], start=True, stop=True)
                ins.then_inc(pEB.s, 1)
                for i in range(14):
                    yield AT_MOE["y"] + i
                    t, h = i // 2, i % 2
                    if i < 2: W(pe, eEB, 1, d)
                    else: W(pe, eY, i - 1, d)
                    pe.matmul(psB[0:TOK_ROWS[t], 512 * h:512 * h + 512], nrmT[:, 2 + 128 * t:2 + 128 * t + TOK_ROWS[t]], ew[:, 512 * h:512 * h + 512], start=True, stop=True).then_inc(pY.s, 1)
                yield AT_LN[1] + LN_AT["turn"]
                ln(1)
                for a, at in ((0, AT_LIN["q"]), (1, AT_LIN["k"])):
                    yield at
                    if a == 0: W(pe, eBT, 2, d)
                    else: W(pe, zm, 1, d)
                    for h in range(2):
                        ins = pe.matmul(psB[:, 512 * h:512 * h + HALF], wqkv[:, 128 * a:128 * a + 128], nrmT[:, 2 + HALF * h:2 + HALF * (h + 1)], start=True, stop=True)
                    ins.then_inc(pQ.s, 1)
                yield AT_LIN["v"]
                W(pe, zm, 2, d)
                for t in tiles:
                    ins = pe.matmul(psB[0:TOK_ROWS[t], 128 * t:128 * t + 128], nrmT[:, 2 + 128 * t:2 + 128 * t + TOK_ROWS[t]], wqkv[:, 256:384], start=True, stop=True)
                ins.then_inc(pV.s, 1)
                for i in tiles:
                    yield AT_LIN["a"] + 2 * i
                    wd, nch, w = width(i)
                    if i == 0: W(pe, qk, 2, d); W(pe, eV, 1, d)
                    elif i < 4: W(pe, eAT, i, d)
                    else: W(pe, eAT, i - 1, d)
                    for h in range(nch):
                        o = 512 * (h if nch == 2 else i % 2)
                        ins = pe.matmul(psB[0:TOK_ROWS[i], o:o + w], kT[:, 128 * i:128 * i + TOK_ROWS[i]], qT[:, 128 * i + w * h:128 * i + w * (h + 1)], start=True, stop=True)
                    ins.then_inc(pAT.s, 1)
                for t in tiles:
                    yield AT_LIN["n"] + t
                    if t == 0: W(pe, eAT, 7, d)
                    if t >= 2: W(pe, eN, t - 1, d)
                    R = TOK_ROWS[t]
                    for i in range(t + 1):
                        ins = pe.matmul(psB[0:R, 512 * (t % 2):512 * (t % 2) + 129], AT[0:TOK_ROWS[i], ATo[i] + 128 * (t - i):ATo[i] + 128 * (t - i) + R], vaug[0:TOK_ROWS[i], i, :], start=(i == 0), stop=(i == t))
                    ins.then_inc(pN.s, 1)
                yield AT_LN[2] + LN_AT["turn"]
                ln(2)
                yield AT_STU["u"]
                W(pe, eBT, 3, d)
                for par in range(2):
                    for i in range(4):
                        c0 = 2 + par + 256 * i; n = ST[i]
                        ins = pe.transpose(psB[0:n, 512 * par + 128 * i:512 * par + 128 * i + 128], nrmT[:, c0:c0 + 2 * n - 1:2], ident[:, :])
                    ins.then_inc(pU.s, 1)
                yield AT_STU["res"]
                W(pe, eU, 2, d)
                transposes(lambda t: tok[0:TOK_ROWS[t], t, :], lambda t: psB[:, 128 * t:128 * t + TOK_ROWS[t]], pR)
                sums2 = lambda lo, hi, t0: psS[:, 1, 1, 0:HALF].rearrange("p (a t) -> p a t", a=2)[:, :, lo - t0:hi - t0]
                def conv(u):
                    half, n = divmod(u, 2 * NK)
                    (t0, t1), _ = HALVES[half]
                    if u == 0: W(pe, eR, 1, d)
                    if u >= 2: W(pe, eC, u - 1, d)
                    tiles_in = [i for i in range(4) if 128 * i < t1]
                    for par in range(2):
                        src = par if n < NK else 1 - par
                        shift = 1 if (n >= NK and par == 0) else 0
                        for i in tiles_in:
                            c0 = max(t0, 128 * i)
                            o = 512 * (u % 2) + QUART * par - t0
                            ins = pe.matmul(psB[:, o + c0:o + t1], U[0:ST[i], src, i, :], toep[0:ST[i], n, 1 - shift + c0 - 128 * i:1 - shift + t1 - 128 * i],
                                            start=(par == 0 and i == 0), stop=(par == 1 and i == tiles_in[-1]), skip_group_check=True)
                    ins.then_inc(pC.s, 1)
                def mixin(u):
                    half, n = divmod(u, 2 * NK)
                    (t0, t1), branches = HALVES[half]
                    W(pe, mix_in[u % MIXES], 16 * (u // MIXES + 1), d)
                    if u == 2 * NK: W(pe, out_ready, 1, d)
                    W(pe, eC, u + 1, d)
                    for s in branches:
                        lo, hi = SEG[s]
                        ins = pe.matmul(sums2(lo, hi, t0), mixr[:, u % MIXES, s, :], UT[:, u % 3, :].rearrange("p (a t) -> p a t", a=2)[:, :, lo - t0:hi - t0],
                                        start=(n == 0 and s == branches[0]), stop=False, skip_group_check=True)
                    ins.then_inc(pZ.s, 1)
                for half in range(2):
                    (t0, t1), branches = HALVES[half]
                    for k in range(2 * NK + 2):
                        yield AT_STU["conv"] + half * (2 * NK + 3) + k
                        if k < 2 * NK: conv(2 * NK * half + k)
                        if k >= 2: mixin(2 * NK * half + k - 2)
                    yield AT_STU["conv"] + half * (2 * NK + 3) + 2 * NK + 2
                    for j in range(3):
                        for s in branches:
                            lo, hi = SEG[s]
                            c0 = 2 - j + 2 * lo
                            ins = pe.matmul(sums2(lo, hi, t0), mixu[:, s, j, :], nrmT[:, c0:c0 + 2 * (hi - lo)].rearrange("p (t a) -> p a t", a=2), start=False, stop=(j == 2), skip_group_check=True)
                    ins.then_inc(pAR.s, 1)

            def run_alone(tracks):
                due = [0] * len(tracks)
                for slot in range(200):
                    in_step(slot, due, tracks)

            def one_pass(b, p, first, last, bb=None):
                tracks = [soft(blk, b, p, last) for blk in range(5)]
                if not first: tracks = [tail(b - 1, 1 - p), rest(b - 1, 1 - p)] + tracks
                if not last: tracks.append(next_image(b + 1, 1 - p))
                due = [0] * len(tracks)
                in_step(-1, due, tracks)
                for pos, blk in enumerate(ORDER):
                    buf = buffer_of(blk)
                    if blk < 6: W(pe, Sev, (-2, 0)[pos] if pos < 2 else pos - 1, b)
                    wd, nch, w = width(blk)
                    for r in range(STEPS if blk < 6 else TAIL):
                        st = STEPS * pos + r
                        if blk < 6:
                            W(pe, th, st + 1, b)
                            for h in range(nch):
                                for q in range(4):
                                    ins = pe.matmul(psS[32 * q:32 * q + 32, buf, h, 0:w], vhot[:, 31 - r:63 - r], ring[:, st % RINGS, q, h * w:(h + 1) * w],
                                                    start=(r == 0), stop=(r == STEPS - 1), skip_group_check=True)
                            ins.then_inc(s_credit, 1)
                            if r == STEPS - 1:
                                pe.matmul(psS[0:32, buf, 0, 504:512], ident[:, 0:32], ident[:, 0:8], start=False, stop=True, skip_group_check=True).then_inc(pS.s, 1)
                            in_step(st, due, tracks)
                        else:
                            if r == 0: W(pe, th, 6 * STEPS + 1, b)
                            ins = pe.matmul(psS[0:32, buf, 0, CORNER_AT:CORNER_AT + TAIL], vhot[:, 31 - r:63 - r], corner[:, TAIL * r:TAIL * (r + 1)], start=(r == 0), stop=(r == TAIL - 1), skip_group_check=True)
                            if r == TAIL - 1: ins.then_inc(pS.s, 1)
                in_step(999, due, tracks)
            passes(pe, lambda: run_alone([next_image(0, 0)]), one_pass, lambda: run_alone([tail(NI - 1, 1), rest(NI - 1, 1)]))

        @block.scalar
        def _(act):
            act.wait_ge(s_set, 2)
            act.activation(sm8[:, 4:8], sm8[:, 0:4], ACT.Exp).then_inc(s_setp, 1)
            act.activation(sg[:, :], sg[:, :], ACT.Sqrt).then_inc(s_setp, 1)
            act.wait_ge(s_setp, 2)
            act.activation(sg[:, :], sg[:, :], ACT.Sqrt).then_inc(s_setp, 1)

            def next_image(b, p):
                proj = proj2[:, p]
                yield AT_NEXT["ln"] + LN_AT["evac"]
                W(act, pBT0, 1, b)
                act.activation(proj[:, :], psA[:, 0:T], ACT.Copy).then_inc(eBT0.s, 1)
                yield AT_NEXT["wiev"]
                W(act, pWi, 1, b)
                act.activation(proj[:, :].rearrange("p (h w) -> p h w", h=2), psA[:, :].rearrange("p (h w) -> p h w", h=2)[:, :, 0:HALF], ACT.Copy).then_inc(eWi.s, 1)
            def exps(blk, b):
                R = TOK_ROWS[blk]
                W(act, mx, blk + 1, b)
                act.activation(S[0:R, blk, :], S[0:R, blk, :], ACT.Exp, bias=small[0:R, blk:blk + 1], accum_out=small[0:R, 8 + blk:9 + blk]).then_inc(ex.s, 1)
            def soft(blk, b):
                yield AT_BLOCK[blk] + AT_SOFT["exp"]
                exps(blk, b)
            def tail(d):
                yield AT_TAIL["exp"]
                exps(5, d)
                exps(6, d)
            def rest(d, q):
                def ln(L):
                    W(act, pBT, L + 1, d)
                    act.activation(nrmT[:, 2:2 + T], psB[:, 0:T], ACT.Copy).then_inc(eBT.s, 1)
                yield AT_LN[0] + LN_AT["evac"]
                ln(0)
                yield AT_MOE["exp"]
                W(act, sub8, 1, d)
                act.activation(prob[:, :, :], logit[:, :, :], ACT.Exp).then_inc(exp8.s, 1)
                yield AT_MOE["evac"]
                W(act, pGT, 1, d)
                act.activation(gateT[:, :], psB[0:8, 0:T], ACT.Copy).then_inc(eGT.s, 1)
                yield AT_LN[1] + LN_AT["evac"]
                ln(1)
                for a, at in ((0, AT_LIN["eq"]), (1, AT_LIN["ek"])):
                    yield at
                    W(act, zm, a + 1, d)
                    act.activation(zmin, zmin, ACT.Exp).then_inc(zexp.s, 1)
                yield AT_LN[2] + LN_AT["evac"]
                ln(2)
                yield AT_STU["uev"]
                W(act, pU, 2, d)
                ps = psB[:, :].rearrange("p (a b c) -> p a b c", a=2, b=4)
                act.activation(U[:, :, 0:3, :], ps[:, :, 0:3, :], ACT.Copy).then_inc(eU.s, 1)
                act.activation(U[0:8, :, 3, :], ps[0:8, :, 3, :], ACT.Copy).then_inc(eU.s, 1)
                yield AT_STU["resev"]
                W(act, pR, 1, d)
                W(act, stored, 16, d - 1)
                act.activation(res[:, :], psB[:, 0:T], ACT.Copy).then_inc(eR.s, 1)
                for u in range(0, 64, 2):
                    yield AT_STU["conv"] + u + u // (2 * NK) * 3 + 1
                    W(act, pC, u + 1, d)
                    if u >= 3: W(act, pZ, u - 2, d)
                    W(act, eC, u, d)
                    act.activation(UT[:, u % 3, :], psB[:, 0:HALF], ACT.Copy).then_inc(eC.s, 1)

            def run_alone(tracks):
                due = [0] * len(tracks)
                for slot in range(200):
                    in_step(slot, due, tracks)

            def one_pass(b, p, first, last, bb=None):
                tracks = [soft(blk, b) for blk in range(5)]
                if not first: tracks = [tail(b - 1), rest(b - 1, 1 - p)] + tracks
                if not last: tracks.append(next_image(b + 1, 1 - p))
                due = [0] * len(tracks)
                for n, track in enumerate(tracks): due[n] = next(track, None)
                for pos, blk in enumerate(ORDER[:6]):
                    wd, nch, w = width(blk)
                    for r in range(STEPS):
                        st = STEPS * pos + r
                        W(act, sums, 4 * (st + 1), b)
                        act.activation(ring[:, st % RINGS, :, 0:wd], ring[:, st % RINGS, :, 0:wd], ACT.Tanh).then_inc(th.s, 1)
                        in_step(st - LEAD_ACT, due, tracks)
                W(act, sums, 4 * 6 * STEPS + 1, b)
                act.activation(corner[:, :], corner[:, :], ACT.Tanh).then_inc(th.s, 1)
                in_step(999, due, tracks)
            passes(act, lambda: run_alone([next_image(0, 0)]), one_pass, lambda: run_alone([tail(NI - 1), rest(NI - 1, 1)]))

        @block.vector
        def _(dve):
            class Chain:
                n = 0; turn = None
                def do(self, ins): self.n += 1; ins.then_inc(dch, 1)
                def sync(self): dve.wait_ge(dch, self.n if self.turn is None else token_layers.K * self.turn + self.n)
                def link(self, ins): self.do(ins); self.sync()
            c = Chain()
            dve.wait_ge(s_pc, 11)
            dve.wait_ge(s_ld, 16 * 14)
            dve.tensor_scalar(vhot[:, :], vhot[:, :], vcol[:, 0:1], None, ALU.mult).then_inc(s_set, 1)
            z, soft_w, hard, rem = lw[:, 8:12], sm8[:, 4:8], lw[:, 0:4], sm8[:, 8:9]
            c.link(dve.tensor_tensor(z, lw[:, 0:4], lw[:, 4:8], ALU.add))
            c.link(dve.tensor_reduce(sm8[:, 9:10], z, AX.X, ALU.max))
            dve.tensor_scalar(sm8[:, 0:4], z, sm8[:, 9:10], None, ALU.subtract).then_inc(s_set, 1)
            dve.wait_ge(s_setp, 3)
            c.link(dve.tensor_reduce(sm8[:, 10:11], soft_w, AX.X, ALU.add))
            c.link(dve.reciprocal(sm8[:, 10:11], sm8[:, 10:11]))
            c.link(dve.tensor_scalar(soft_w, soft_w, sm8[:, 10:11], None, ALU.mult))
            c.link(dve.tensor_reduce(sm8[:, 11:12], soft_w, AX.X, ALU.max))
            c.link(dve.tensor_scalar(hard, soft_w, sm8[:, 11:12], None, ALU.is_equal))
            c.link(dve.memset(rem, 1.0))
            for i in range(4):
                c.link(dve.tensor_tensor(hard[:, i:i + 1], hard[:, i:i + 1], rem, ALU.mult))
                c.link(dve.tensor_tensor(rem, rem, hard[:, i:i + 1], ALU.subtract))
            c.link(dve.tensor_tensor(hard, hard, soft_w, ALU.subtract))
            c.link(dve.tensor_tensor(hard, hard, soft_w, ALU.add))
            for i in range(4):
                c.do(dve.tensor_scalar(coef[:, i, :], sg[:, :], hard[:, i:i + 1], None, ALU.mult))
            c.sync()
            for i in range(4):
                dve.wait_ge(s_br, 48 * (i + 1))
                c.do(dve.tensor_tensor(msum, mp, mm_, ALU.add))
                c.do(dve.tensor_tensor(mdif, mp, mm_, ALU.subtract))
                if i == 0:
                    c.do(dve.tensor_scalar(mixu[:, 0, :, :], mu, hard[:, 0:1], None, ALU.mult))
                else:
                    flat = lambda a: a.rearrange("p a b -> p (a b)")
                    c.do(dve.scalar_tensor_tensor(out=flat(mixu[:, i, :, :]), in0=flat(mu), scalar=hard[:, i:i + 1], in1=flat(mixu[:, i - 1, :, :]), op0=ALU.mult, op1=ALU.add))
                c.sync()
                dve.memset(pad[:, 7:8], 0.0).then_inc(s_brf, 1)
                if i: dve.wait_ge(s_mst, 16 * i)
                dve.wait_ge(s_brf, i + 1)
                for k in range(NK):
                    for eo, m in enumerate((msum, mdif)):
                        dst = mrun.rearrange("p a b c -> p (a b) c")[:, NK * eo + k, :]
                        if i == 0:
                            c.do(dve.tensor_scalar(dst, m[:, k, :], coef[:, 0, k:k + 1], None, ALU.mult))
                        else:
                            c.do(dve.scalar_tensor_tensor(out=dst, in0=m[:, k, :], scalar=coef[:, i, k:k + 1], in1=dst, op0=ALU.mult, op1=ALU.add))
                c.sync()
                dve.memset(pad[:, 6:7], 0.0).then_inc(s_mrun, 1)
                dve.wait_ge(s_mrun, i + 1)

            def evac(blk, b):
                R = TOK_ROWS[blk]; wd, nch, w = width(blk)
                W(dve, pS, min(POS[blk] + 1, 7) if blk < 5 else 7, b)
                o = CORNER_AT if blk == 6 else 0
                dve.tensor_copy(S[0:R, blk, 128 * blk:T].rearrange("p (h w) -> p h w", h=nch), psS[0:R, buffer_of(blk), 0:nch, o:o + w]).then_inc(Sev.s, 1)
            def evacs(b):
                for pos, blk in enumerate(ORDER[:5]):
                    yield STEPS * (pos + 1) + AT_EVAC
                    evac(blk, b)
            def filled(blk, b):
                W(dve, pF, blk + 1, b)
                if blk < 5:
                    c.link(dve.tensor_copy(S[:, blk + 1:6, 128 * blk:128 * blk + 128], psA[:, 0:128 * (5 - blk)].rearrange("p (t c) -> p t c", c=128)))
                dve.tensor_copy(S[0:TAIL, 6, 128 * blk:128 * blk + 128], psA[0:TAIL, 128 * (5 - blk):128 * (6 - blk)]).then_inc(eF.s, 1)
            def rowmax(blk, b):
                R = TOK_ROWS[blk]
                W(dve, Sev, POS[blk] + 1, b)
                W(dve, eF, min(blk + 1, 6), b)
                dve.tensor_reduce(small[0:R, blk:blk + 1], S[0:R, blk, :], AX.X, ALU.max, negate=True).then_inc(mx.s, 1)
            def scale(blk, b):
                R = TOK_ROWS[blk]
                W(dve, ex, blk + 1, b)
                c.link(dve.reciprocal(small[0:R, 16 + blk:17 + blk], small[0:R, 8 + blk:9 + blk]))
                dve.tensor_scalar(S[0:R, blk, :], S[0:R, blk, :], small[0:R, 16 + blk:17 + blk], None, ALU.mult).then_inc(eP.s, 1)
            def turned(blk, b):
                R = TOK_ROWS[blk]
                W(dve, pPT, blk + 1, b)
                c.link(dve.tensor_copy(PT[:, 0:6, 0:R], psA[:, 0:6 * R].rearrange("p (t c) -> p t c", c=R)))
                dve.tensor_copy(PT[0:TAIL, 6, 0:R], psA[0:TAIL, 6 * R:7 * R]).then_inc(ePT.s, 1)
            def add_attended(blk, b, tok):
                R = TOK_ROWS[blk]
                W(dve, pO, blk + 1, b)
                dve.tensor_tensor(tok[0:R, blk, :], tok[0:R, blk, :], psA[0:R, 896:1024], ALU.add).then_inc(eO.s, 1)
            def soft(blk, b, p):
                s0 = AT_BLOCK[blk]
                yield s0 + AT_SOFT["rowmax"]
                filled(blk, b); rowmax(blk, b)
                yield s0 + AT_SOFT["scale"]
                scale(blk, b)
                yield s0 + AT_SOFT["ptev"]
                turned(blk, b)
                yield s0 + AT_SOFT["add"]
                add_attended(blk, b, tok2[:, p])
            def tail(d, q):
                tok = tok2[:, q]
                yield AT_TAIL["evac"]
                evac(5, d); evac(6, d)
                yield AT_TAIL["rowmax"]
                filled(5, d); rowmax(5, d); rowmax(6, d)
                yield AT_TAIL["scale"]
                scale(5, d); scale(6, d)
                yield AT_TAIL["ptev5"]
                turned(5, d)
                yield AT_TAIL["add5"]
                add_attended(5, d, tok); turned(6, d)
                yield AT_TAIL["add6"]
                add_attended(6, d, tok)
                W(dve, eO, 7, d)

            def ln(at, tok, nrm, d, k, evs):
                ready, rooted, done = evs
                yield at + LN_AT["stats"]
                for t in tiles: c.do(dve.bn_stats(stats[:, t, :], tok[:, t, :]))
                yield at + LN_AT["aggr"]
                c.sync()
                c.do(dve.memset(pad[:, 0:1], 0.0))
                for t in tiles: c.do(dve.bn_aggr(mv[:, t, :], stats[:, t, :]))
                c.sync()
                dve.tensor_scalar(var[:, :], mv[:, :, 1], LN_EPS, None, ALU.add).then_inc(ready.s, 1)
                yield at + LN_AT["norm"]
                W(dve, rooted, k, d)
                for t in tiles:
                    ins = dve.tensor_scalar(nrm[:, t, :], tok[:, t, :], mv[:, t, 0:1], rstd[:, t:t + 1], ALU.subtract, ALU.mult)
                    if t < 6: c.do(ins)
                c.sync()
                ins.then_inc(done.s, 1)
            def next_image(b, p):
                tok, nrm = tok2[:, p], nrm2[:, p]
                yield AT_NEXT["tok"]
                W(dve, pX, 1, b)
                dve.tensor_copy(tok[:, 0:6, :], psA[:, 0:768].rearrange("p (t c) -> p t c", c=128)).then_inc(tT.s, 1)
                dve.tensor_copy(tok[0:TAIL, 6, :], psA[0:TAIL, 768:896]).then_inc(tT.s, 1)
                W(dve, tT, 2, b)
                c.do(dve.memset(pad[:, 1:2], 0.0))
                yield from ln(AT_NEXT["ln"], tok, nrm, b, 1, (lnv0, lns0, lnB0))

            def rest(d, q):
                tok, nrm = tok2[:, q], nrm2[:, q]
                yield from ln(AT_LN[0], tok, nrm, d, 1, (lnv, lns, lnB))
                yield AT_MOE["bias_add"]
                W(dve, pL, 1, d)
                pl = psB[:, 0:56].rearrange("p (t e) -> p t e", e=8)
                rbb = rb[:, :].unsqueeze(1).to_broadcast([128, 6, 8])
                c.do(dve.memset(logit[:, 6, :], 0.0))
                c.sync()
                c.do(dve.tensor_tensor(logit[:, 0:6, :], pl[:, 0:6, :], rbb, ALU.add))
                c.do(dve.tensor_tensor(logit[0:TAIL, 6, :], pl[0:TAIL, 6, :], rb[0:TAIL, :], ALU.add))
                c.sync()
                c.link(dve.tensor_reduce(small[:, 24:31], logit[:, :, :], AX.X, ALU.max))
                bc = lambda a: a.unsqueeze(2).to_broadcast([128, NT, 8])
                dve.tensor_tensor(logit[:, :, :], logit[:, :, :], bc(small[:, 24:31]), ALU.subtract).then_inc(sub8.s, 1)
                yield AT_MOE["rank"]
                W(dve, exp8, 1, d)
                c.link(dve.tensor_reduce(small[:, 32:39], prob[:, :, :], AX.X, ALU.add))
                c.link(dve.reciprocal(small[:, 32:39], small[:, 32:39]))
                c.link(dve.tensor_tensor(prob[:, :, :], prob[:, :, :], bc(small[:, 32:39]), ALU.mult))
                mine = prob[:, :, :].unsqueeze(3).to_broadcast([128, NT, 8, 8]); other = prob[:, :, :].unsqueeze(2).to_broadcast([128, NT, 8, 8])
                c.do(dve.tensor_tensor(gt[:, :, :, :], other, mine, ALU.is_gt))
                yield AT_MOE["rank2"]
                c.link(dve.tensor_tensor(eq[:, :, :, :], other, mine, ALU.is_equal))
                c.link(dve.tensor_tensor(eq[:, :, :, :], eq[:, :, :, :], lower[:, :, :].unsqueeze(1).to_broadcast([128, NT, 8, 8]), ALU.mult))
                c.link(dve.tensor_tensor(gt[:, :, :, :], gt[:, :, :, :], eq[:, :, :, :], ALU.add))
                yield AT_MOE["gate"]
                c.link(dve.tensor_reduce(logit[:, :, :], gt[:, :, :, :], AX.X, ALU.add))
                c.link(dve.tensor_scalar(logit[:, :, :], logit[:, :, :], 2.0, None, ALU.is_lt))
                c.link(dve.tensor_tensor(prob[:, :, :], prob[:, :, :], logit[:, :, :], ALU.mult))
                c.link(dve.tensor_reduce(small[:, 40:47], prob[:, :, :], AX.X, ALU.add))
                c.link(dve.reciprocal(small[:, 40:47], small[:, 40:47]))
                dve.tensor_tensor(prob[:, :, :], prob[:, :, :], bc(small[:, 40:47]), ALU.mult).then_inc(gate.s, 1)
                yield AT_MOE["bias_used"]
                W(dve, pEB, 1, d)
                c.do(dve.tensor_tensor(tok[:, 0:6, :], tok[:, 0:6, :], psB[:, 0:768].rearrange("p (t c) -> p t c", c=128), ALU.add))
                c.sync()
                dve.tensor_tensor(tok[0:TAIL, 6, :], tok[0:TAIL, 6, :], psB[0:TAIL, 768:896], ALU.add).then_inc(eEB.s, 1)
                W(dve, gate, 1, d)
                W(dve, eEB, 1, d)
                for i in range(14):
                    yield AT_MOE["y"] + i + 1
                    t, h = i // 2, i % 2
                    R = TOK_ROWS[t]
                    W(dve, pY, i + 1, d)
                    if i: W(dve, eY, i, d)
                    for e in range(4):
                        ins = dve.scalar_tensor_tensor(out=tok[0:R, t, :], in0=psB[0:R, 512 * h + 128 * e:512 * h + 128 * e + 128], scalar=prob[0:R, t, 4 * h + e:4 * h + e + 1], in1=tok[0:R, t, :], op0=ALU.mult, op1=ALU.add)
                        if e < 3: c.link(ins)
                    ins.then_inc(eY.s, 1)
                W(dve, eY, 14, d)
                c.do(dve.memset(pad[:, 2:3], 0.0))
                yield from ln(AT_LN[1], tok, nrm, d, 2, (lnv, lns, lnB))
                v2 = lambda x: x.rearrange("p (h w) -> p h w", h=2)
                for a, at_z, at_out in ((0, AT_LIN["zq"], AT_LIN["qout"]), (1, AT_LIN["zk"], AT_LIN["kout"])):
                    yield at_z
                    W(dve, pQ, a + 1, d)
                    c.link(dve.tensor_scalar(v2(zq), psB[:, :].rearrange("p (h w) -> p h w", h=2)[:, :, 0:HALF], bqk[:, a:a + 1], None, ALU.add))
                    dve.tensor_scalar(zmin, zq, 0.0, None, ALU.min).then_inc(zm.s, 1)
                    yield at_out
                    W(dve, zexp, a + 1, d)
                    dve.scalar_tensor_tensor(out=(qT, kT)[a], in0=zq, scalar=0.0, in1=zmin, op0=ALU.max, op1=ALU.add).then_inc(qk.s, 1)
                    W(dve, qk, a + 1, d)
                yield AT_LIN["vout"]
                W(dve, pV, 1, d)
                c.do(dve.tensor_tensor(vaug[:, 0:6, 0:128], psB[:, 0:768].rearrange("p (t c) -> p t c", c=128), bv[:, :].unsqueeze(1).to_broadcast([128, 6, 128]), ALU.add))
                c.do(dve.memset(vaug[:, :, 128:129], 1.0))
                c.sync()
                dve.tensor_tensor(vaug[0:TAIL, 6, 0:128], psB[0:TAIL, 768:896], bv[0:TAIL, :], ALU.add).then_inc(eV.s, 1)
                for i in tiles:
                    yield AT_LIN["a"] + 2 * i + 1
                    R = TOK_ROWS[i]; wd, nch, w = width(i)
                    W(dve, pAT, i + 1, d)
                    o = 0 if nch == 2 else 512 * (i % 2)
                    src = psB[0:R, :].rearrange("p (h w) -> p h w", h=2)[:, :, 0:w] if nch == 2 else psB[0:R, o:o + w].unsqueeze(1)
                    c.link(dve.tensor_copy(AT[0:R, ATo[i]:ATo[i] + wd].rearrange("p (h w) -> p h w", h=nch), src))
                    dve.tensor_tensor(AT[0:R, ATo[i]:ATo[i] + R], AT[0:R, ATo[i]:ATo[i] + R], causal[0:R, 0:R], ALU.mult).then_inc(eAT.s, 1)
                for t in tiles:
                    yield AT_LIN["n"] + t + 1
                    R = TOK_ROWS[t]; o = 512 * (t % 2)
                    W(dve, pN, t + 1, d)
                    c.link(dve.tensor_scalar(small[0:R, 48 + t:49 + t], psB[0:R, o + 128:o + 129], 1e-6, None, ALU.add))
                    c.link(dve.reciprocal(small[0:R, 48 + t:49 + t], small[0:R, 48 + t:49 + t]))
                    dve.scalar_tensor_tensor(out=tok[0:R, t, :], in0=psB[0:R, o:o + 128], scalar=small[0:R, 48 + t:49 + t], in1=tok[0:R, t, :], op0=ALU.mult, op1=ALU.add).then_inc(eN.s, 1)
                W(dve, eN, 7, d)
                c.do(dve.memset(pad[:, 3:4], 0.0))
                yield from ln(AT_LN[2], tok, nrm, d, 3, (lnv, lns, lnB))
                for u in range(1, 64, 2):
                    yield AT_STU["conv"] + u + u // (2 * NK) * 3 + 1
                    W(dve, pC, u + 1, d)
                    W(dve, eC, u, d)
                    if u >= 3: W(dve, pZ, u - 2, d)
                    dve.tensor_copy(UT[:, u % 3, :], psB[:, 512:512 + HALF]).then_inc(eC.s, 1)
                    if u % (2 * NK) == 2 * NK - 1:
                        half = u // (2 * NK); t0, t1 = HALVES[half][0]
                        yield AT_STU["conv"] + half * (2 * NK + 3) + 2 * NK + 3
                        W(dve, eR, 1, d)
                        W(dve, pAR, half + 1, d)
                        r2 = res[:, 2 * t0:2 * t1].rearrange("p (t a) -> p a t", a=2)
                        dve.tensor_tensor(r2, r2, psS[:, 1, 1, 0:HALF].rearrange("p (a t) -> p a t", a=2), ALU.add).then_inc(out_ready.s, 1)
                W(dve, out_ready, 2, d)

            def run_alone(tracks):
                due = [0] * len(tracks)
                for slot in range(-1, 200):
                    in_step(slot, due, tracks)

            seen = {}
            def one_pass(b, p, first, last, bb=None):
                if bb is not None and c.turn is None: c.turn = bb; seen["at"] = c.n
                if bb is None and c.turn is not None:
                    K = c.n - seen["at"]
                    assert K == token_layers.K, K
                    c.turn = None; c.n = seen["at"] + K * ((NI - 2) // 2)
                proj = proj2[:, p]
                tracks = [evacs(b)] + [soft(blk, b, p) for blk in range(5)]
                if not first: tracks = [tail(b - 1, 1 - p), rest(b - 1, 1 - p)] + tracks
                if not last: tracks.append(next_image(b + 1, 1 - p))
                due = [0] * len(tracks)
                for n, track in enumerate(tracks): due[n] = next(track, None)
                W(dve, eWi, 1, b)
                for pos, blk in enumerate(ORDER[:6]):
                    wd, nch, w = width(blk)
                    for r in range(STEPS):
                        st = STEPS * pos + r
                        dve.wait_ge(s_credit, 6 * STEPS * b + st + 1)
                        for q in range(4):
                            i = 128 * blk + 32 * q + r
                            dve.tensor_scalar(ring[:, st % RINGS, q, 0:wd], proj[:, 128 * blk:T], proj[:, i:i + 1], None, ALU.add).then_inc(sums.s, 1)
                        in_step(st - LEAD_DVE, due, tracks)
                pj = proj[:, T - TAIL:T]
                dve.tensor_tensor(corner[:, :].rearrange("p (a b) -> p a b", a=TAIL), pj.unsqueeze(1).to_broadcast([128, TAIL, TAIL]), pj.unsqueeze(2).to_broadcast([128, TAIL, TAIL]), ALU.add).then_inc(sums.s, 1)
                in_step(999, due, tracks)
            passes(dve, lambda: run_alone([next_image(0, 0)]), one_pass, lambda: run_alone([tail(NI - 1, 1), rest(NI - 1, 1)]))
token_layers.K = 380


def build(nc, ai, out, pairs):
    x1 = nc.dram_tensor("x1_scratch", (pairs, 2, 128, T), F32, kind="Internal").ap()
    conv_layers(nc, ai, x1, pairs)
    token_layers(nc, ai, x1.rearrange("p i c t -> (p i) c t"), out, 2 * pairs)

def kernel(**inputs):
    import numpy as _np
    import concourse.bacc as _bacc
    from concourse import mybir as _mybir
    from concourse.bass_utils import run_bass_kernel_spmd as _run

    v = {k: _np.asarray(a) for k, a in inputs.items()}
    taps = lambda w: w.reshape(128, 128, 9).transpose(1, 2, 0)
    phi = _np.zeros((2, 16, 128 + HALF), _np.float32)
    phi[:, :, 128:] = v["L3_ffn_phi"][:T].reshape(HALF, 2, 16).transpose(1, 2, 0)
    toep = phi.reshape(32, 128 + HALF)[:, 127 - _np.arange(128)[:, None] + _np.arange(HALF + 1)[None, :]].transpose(1, 0, 2)
    data = {
        "x": v["x"].reshape(8, 2, 128, T),
        "w0t": v["L0_conv_W"].reshape(4, 32, 128, 9).transpose(2, 3, 1, 0).reshape(128, 9, 128),
        "w0r": v["L0_conv_W"].reshape(128, -1),
        "w1t": taps(v["L1_conv_w1"]), "w2t": taps(v["L1_conv_w2"]),
        "gamma1": v["L1_conv_gamma1"], "gamma2": v["L1_conv_gamma2"], "beta1": v["L1_conv_beta1"], "beta2": v["L1_conv_beta2"],
        "mean1": v["L1_conv_mean1"], "mean2": v["L1_conv_mean2"], "var1": v["L1_conv_var1"], "var2": v["L1_conv_var2"],
        "wa": v["L2_attn_W"].T, "v": v["L2_attn_v"], "rw": v["L2_ffn_router_w"], "rb": v["L2_ffn_router_b"],
        "ew": v["L2_ffn_expert_w"].transpose(1, 0, 2).reshape(128, 1024), "eb": v["L2_ffn_expert_b"],
        "wqkv": v["L3_attn_W"].T, "bqkv": v["L3_attn_b"],
        "sigma": v["L3_ffn_sigma"], "lw": v["L3_ffn_log_weights"], "gum": v["L3_ffn_gumbel"], "toep": toep,
        "mp": v["L3_ffn_M_phi_plus"], "mm": v["L3_ffn_M_phi_minus"], "mu": v["L3_ffn_M_u"],
    }
    nc = _bacc.Bacc("TRN2", target_bir_lowering=False, num_devices=1)
    arrays, aps = {}, {}
    for name, a in data.items():
        a = _np.ascontiguousarray(a)
        arrays[f"in_{name}_dram"] = a
        aps[name] = nc.dram_tensor(f"in_{name}_dram", a.shape, _mybir.dt.from_np(a.dtype), kind="ExternalInput").ap()
    out = nc.dram_tensor("out_0_dram", (16, 128, T), _mybir.dt.float32, kind="ExternalOutput").ap()
    build(nc, aps, out, 8)
    r = _run(nc, [arrays], core_ids=[0])
    return r.results[0]["out_0_dram"].reshape(16, 128, 28, 28)
```
